# Optimizing a Trainium2 kernel written in Bass

```python
import numpy as np
import jax
import jax.numpy as jnp

def _softmax(x, axis=-1):
    return jax.nn.softmax(x, axis=axis)

def _gelu(x):
    return jax.nn.gelu(x, approximate=True)

def _silu(x):
    return jax.nn.silu(x)

def _sigmoid(x):
    return jax.nn.sigmoid(x)

def _layernorm(x, axis=-1, eps=1e-05):
    m = jnp.mean(x, axis=axis, keepdims=True)
    v = jnp.var(x, axis=axis, keepdims=True)
    return (x - m) / jnp.sqrt(v + eps)

def _scatter_add(tgt, idx, src, axis=0):
    return tgt.at[idx].add(src)

def _segment_sum(src, seg, n):
    return jax.ops.segment_sum(src, seg, n)
kernel_name = 'mk_seq_preln_d2_jaxref_r4_3c6320'

def setup_inputs(seed: int=0):
    np.random.seed(seed)
    _w = jnp.asarray

    def _L0_attn_setup():
        import jax, jax.numpy as jnp
        import numpy as np
        N_HEAD = 16

        def _phi(x):
            return jax.nn.silu(x) + 1.0
        key = jax.random.key(seed)
        ks = jax.random.split(key, 8)
        B, T, D = (8, 1024, 256)
        s = 0.02
        return {'x': jax.random.normal(ks[0], (B, T, D), jnp.float32), 'Wq': jax.random.normal(ks[1], (D, D), jnp.float32) * s, 'bq': jax.random.normal(ks[2], (D,), jnp.float32) * s, 'Wk': jax.random.normal(ks[3], (D, D), jnp.float32) * s, 'Wv': jax.random.normal(ks[4], (D, D), jnp.float32) * s, 'bv': jax.random.normal(ks[5], (D,), jnp.float32) * s, 'Wo': jax.random.normal(ks[6], (D, D), jnp.float32) * s, 'bo': jax.random.normal(ks[7], (D,), jnp.float32) * s}
    _L0_attn_in = _L0_attn_setup()

    def _L0_ffn_setup():
        import jax, jax.numpy as jnp
        import numpy as np
        D_IN, D_HID = (256, 1024)

        def _ternary(key, shape):
            return jax.random.randint(key, shape, -1, 2).astype(jnp.float32)

        def _tlin(x, w, s):
            return jnp.einsum('bsi,oi->bso', x, w) * s
        key = jax.random.key(seed)
        ks = jax.random.split(key, 12)
        inv = lambda fan: 1.0 / np.sqrt(fan).astype(np.float32)
        return {'x': jax.random.normal(ks[0], (4, 512, D_IN), dtype=jnp.float32), 'w1_w': _ternary(ks[1], (D_HID, D_IN)), 'w1_s': jax.random.uniform(ks[2], (D_HID,), dtype=jnp.float32) * inv(D_IN), 'w2_w': _ternary(ks[3], (D_HID, D_IN)), 'w2_s': jax.random.uniform(ks[4], (D_HID,), dtype=jnp.float32) * inv(D_IN), 'h1_w': _ternary(ks[5], (D_HID, D_HID)), 'h1_s': jax.random.uniform(ks[6], (D_HID,), dtype=jnp.float32) * inv(D_HID), 'h2_w': _ternary(ks[7], (D_HID, D_HID)), 'h2_s': jax.random.uniform(ks[8], (D_HID,), dtype=jnp.float32) * inv(D_HID), 'w3_w': _ternary(ks[9], (D_IN, D_HID)), 'w3_s': jax.random.uniform(ks[10], (D_IN,), dtype=jnp.float32) * inv(D_HID)}
    _L0_ffn_in = _L0_ffn_setup()

    def _L1_attn_setup():
        import jax, jax.numpy as jnp
        import numpy as np
        EMBED_DIM = 256
        key = jax.random.key(seed)
        ks = jax.random.split(key, 9)
        B, S, D = (4, 1024, EMBED_DIM)
        s = 1.0 / np.sqrt(D)
        inp = {'x': jax.random.normal(ks[0], (B, S, D), dtype=jnp.float32)}
        names = ['q', 'k', 'v', 'out']
        for i, n in enumerate(names):
            inp[f'w_{n}'] = jax.random.uniform(ks[1 + 2 * i], (D, D), jnp.float32, -s, s)
            inp[f'b_{n}'] = jax.random.uniform(ks[2 + 2 * i], (D,), jnp.float32, -s, s)
        return inp
    _L1_attn_in = _L1_attn_setup()

    def _L1_ffn_setup():
        import jax, jax.numpy as jnp
        import numpy as np
        D_MODEL = 256
        key = jax.random.key(seed)
        k_x, k_w, k_a1, k_a2 = jax.random.split(key, 4)
        x = jax.random.normal(k_x, (4, 512, D_MODEL), dtype=jnp.float32)
        weight = jax.random.normal(k_w, (D_MODEL, D_MODEL), dtype=jnp.float32) * 0.02
        aux_weight1 = jax.random.normal(k_a1, (D_MODEL, D_MODEL), dtype=jnp.float32) * 0.02
        aux_weight2 = jax.random.normal(k_a2, (D_MODEL, D_MODEL), dtype=jnp.float32) * 0.02
        bias = jnp.zeros((D_MODEL,), dtype=jnp.float32)
        return {'x': x, 'weight': weight, 'aux_weight1': aux_weight1, 'aux_weight2': aux_weight2, 'bias': bias}
    _L1_ffn_in = _L1_ffn_setup()
    _d = {'L0_attn_x': _L0_attn_in['x'], 'L0_attn_Wq': _L0_attn_in['Wq'], 'L0_attn_bq': _L0_attn_in['bq'], 'L0_attn_Wk': _L0_attn_in['Wk'], 'L0_attn_Wv': _L0_attn_in['Wv'], 'L0_attn_bv': _L0_attn_in['bv'], 'L0_attn_Wo': _L0_attn_in['Wo'], 'L0_attn_bo': _L0_attn_in['bo'], 'L0_ffn_w1_w': _L0_ffn_in['w1_w'], 'L0_ffn_w1_s': _L0_ffn_in['w1_s'], 'L0_ffn_w2_w': _L0_ffn_in['w2_w'], 'L0_ffn_w2_s': _L0_ffn_in['w2_s'], 'L0_ffn_h1_w': _L0_ffn_in['h1_w'], 'L0_ffn_h1_s': _L0_ffn_in['h1_s'], 'L0_ffn_h2_w': _L0_ffn_in['h2_w'], 'L0_ffn_h2_s': _L0_ffn_in['h2_s'], 'L0_ffn_w3_w': _L0_ffn_in['w3_w'], 'L0_ffn_w3_s': _L0_ffn_in['w3_s'], 'L1_attn_w_q': _L1_attn_in['w_q'], 'L1_attn_b_q': _L1_attn_in['b_q'], 'L1_attn_w_k': _L1_attn_in['w_k'], 'L1_attn_b_k': _L1_attn_in['b_k'], 'L1_attn_w_v': _L1_attn_in['w_v'], 'L1_attn_b_v': _L1_attn_in['b_v'], 'L1_attn_w_out': _L1_attn_in['w_out'], 'L1_attn_b_out': _L1_attn_in['b_out'], 'L1_ffn_weight': _L1_ffn_in['weight'], 'L1_ffn_aux_weight1': _L1_ffn_in['aux_weight1'], 'L1_ffn_aux_weight2': _L1_ffn_in['aux_weight2'], 'L1_ffn_bias': _L1_ffn_in['bias']}
    _x0 = _d['L0_attn_x']
    _d['L0_attn_x'] = jax.random.normal(jax.random.fold_in(jax.random.key(seed), 1), (16, 512, 256), dtype=_x0.dtype)
    del _x0
    return _d

def reference(L0_attn_x, L0_attn_Wq, L0_attn_bq, L0_attn_Wk, L0_attn_Wv, L0_attn_bv, L0_attn_Wo, L0_attn_bo, L0_ffn_w1_w, L0_ffn_w1_s, L0_ffn_w2_w, L0_ffn_w2_s, L0_ffn_h1_w, L0_ffn_h1_s, L0_ffn_h2_w, L0_ffn_h2_s, L0_ffn_w3_w, L0_ffn_w3_s, L1_attn_w_q, L1_attn_b_q, L1_attn_w_k, L1_attn_b_k, L1_attn_w_v, L1_attn_b_v, L1_attn_w_out, L1_attn_b_out, L1_ffn_weight, L1_ffn_aux_weight1, L1_ffn_aux_weight2, L1_ffn_bias):

    def _L0_attn_ref(x, Wq, bq, Wk, Wv, bv, Wo, bo):
        import jax, jax.numpy as jnp
        import numpy as np
        N_HEAD = 16

        def _phi(x):
            return jax.nn.silu(x) + 1.0
        B, T, D = x.shape
        H = N_HEAD
        Dh = D // H
        scale = Dh ** (-0.25)
        q = x @ Wq.T + bq
        k = x @ Wk.T
        v = x @ Wv.T + bv
        q = q.reshape(B, T, H, Dh).transpose(0, 2, 1, 3) * scale
        k = k.reshape(B, T, H, Dh).transpose(0, 2, 1, 3) * scale
        v = v.reshape(B, T, H, Dh).transpose(0, 2, 1, 3)
        phi_q = _phi(q)
        phi_k = _phi(k)
        kv = jnp.einsum('bhtd,bhte->bhde', phi_k, v)
        out = jnp.einsum('bhtd,bhde->bhte', phi_q, kv)
        wv = out.transpose(0, 2, 1, 3).reshape(B, T, D)
        return wv @ Wo.T + bo

    def _L0_ffn_ref(x, w1_w, w1_s, w2_w, w2_s, h1_w, h1_s, h2_w, h2_s, w3_w, w3_s):
        import jax, jax.numpy as jnp
        import numpy as np
        D_IN, D_HID = (256, 1024)

        def _ternary(key, shape):
            return jax.random.randint(key, shape, -1, 2).astype(jnp.float32)

        def _tlin(x, w, s):
            return jnp.einsum('bsi,oi->bso', x, w) * s
        h = jax.nn.silu(_tlin(x, w1_w, w1_s)) * _tlin(x, w2_w, w2_s)
        h = jax.nn.gelu(_tlin(h, h1_w, h1_s), approximate=False)
        h = jax.nn.gelu(_tlin(h, h2_w, h2_s), approximate=False)
        return _tlin(h, w3_w, w3_s)

    def _L1_attn_ref(x, w_q, b_q, w_k, b_k, w_v, b_v, w_out, b_out):
        import jax, jax.numpy as jnp
        import numpy as np
        EMBED_DIM = 256
        D = x.shape[-1]
        scaling = 1.0 / jnp.sqrt(jnp.asarray(D, x.dtype))
        q = jnp.einsum('bsd,ed->bse', x, w_q) + b_q
        k = jnp.einsum('bsd,ed->bse', x, w_k) + b_k
        v = jnp.einsum('bsd,ed->bse', x, w_v) + b_v
        scores = jnp.einsum('bqd,bkd->bqk', q, k) * scaling
        attn = jax.nn.softmax(scores, axis=-1)
        out = jnp.einsum('bqk,bkd->bqd', attn, v)
        return jnp.einsum('bsd,ed->bse', out, w_out) + b_out

    def _L1_ffn_ref(x, weight, aux_weight1, aux_weight2, bias):
        import jax, jax.numpy as jnp
        import numpy as np
        D_MODEL = 256
        h = jnp.einsum('btc,cd->btd', x, weight)
        h = jnp.einsum('btc,cd->btd', h, aux_weight1)
        h = jnp.einsum('btc,cd->btd', h, aux_weight2)
        return jnp.tanh(h + bias)
    x = L0_attn_x
    x = x + _L0_attn_ref(_layernorm(x, axis=-1), L0_attn_Wq, L0_attn_bq, L0_attn_Wk, L0_attn_Wv, L0_attn_bv, L0_attn_Wo, L0_attn_bo)
    x = x + _L0_ffn_ref(_layernorm(x, axis=-1), L0_ffn_w1_w, L0_ffn_w1_s, L0_ffn_w2_w, L0_ffn_w2_s, L0_ffn_h1_w, L0_ffn_h1_s, L0_ffn_h2_w, L0_ffn_h2_s, L0_ffn_w3_w, L0_ffn_w3_s)
    x = x + _L1_attn_ref(_layernorm(x, axis=-1), L1_attn_w_q, L1_attn_b_q, L1_attn_w_k, L1_attn_b_k, L1_attn_w_v, L1_attn_b_v, L1_attn_w_out, L1_attn_b_out)
    x = x + _L1_ffn_ref(_layernorm(x, axis=-1), L1_ffn_weight, L1_ffn_aux_weight1, L1_ffn_aux_weight2, L1_ffn_bias)
    return x

_drawn_inputs = setup_inputs


def setup_inputs(seed=0):
    import zlib

    import numpy as np

    out = dict(_drawn_inputs(seed))
    spreads = {'L1_ffn_bias': (0.0, 0.1)}
    factors = {}
    for name, (base, spread) in spreads.items():
        noise = np.random.default_rng([zlib.crc32(name.encode()), seed]).standard_normal(out[name].shape)
        drawn = base * np.exp(spread * noise) if base else spread * noise
        out[name] = jnp.asarray(drawn.astype(out[name].dtype))
    for name, factor in factors.items():
        out[name] = (out[name] * factor).astype(out[name].dtype)
    return out
```

```python
from contextlib import ExitStack

import numpy as np
import concourse.bass as bass
from concourse import mybir

F32 = mybir.dt.float32
F32R = mybir.dt.float32r
U32 = mybir.dt.uint32
I32 = mybir.dt.int32
ALU = mybir.AluOpType
ACT = mybir.ActivationFunctionType
AX = mybir.AxisListType

P = 128
D = 256
KD = D // P
HID = 1024
KH = HID // P
S = 512
NB = S // P
T = 16
HEAD = 16
HT = S // 2
HB = HT // P
PAIRS = KH // 2
SLOTS = 4
RING = 4
EPS = 1e-5
LOWBITS = 0xFFF
CHUNK = 512

LN = {"ln_stats": 3, "ln_pow": 1, "xn_ready": 1}
ADDS = {
    "U": {"ffn_fill": 2, "hi_ready": 1, "ffn_ready": 1},
    "G": {"ffn_fill": 1, "hi_ready": 1, "ffn_ready": 1},
    "H": {"ffn_fill": 1, "hi_ready": 1, "ffn_ready": 1},
    "W": {"ffn_fill": 1, "b_done": 1},
    "BL": LN,
    "BT": {"ffn_fill": 1, "bt_hi": 1},
    "AL": {**LN, "bias_added": 1, "a_tile": 1},
    "CL": {**LN, "bias_added": 1, "key_bias": 2},
    "CL2": LN,
    "T": {"att_fill": 2},
    "AKV": {"att_fill": 1, "k_silu": 1, "phik_ready": 1},
    "AQ": {"att_fill": 2, "phiq_ready": 2},
    "AS": {"att_fill": 1},
    "AM": {"att_fill": 1},
    "AO": {"att_fill": 2},
    "CV": {"att_fill": 2},
    "CZ": {"att_fill": 2},
    "CS": {"att_fill": 1, "row_max": 2, "exp_bias": 1},
    "CP": {"att_fill": 1},
    "CO": {"att_fill": 1, "inverse": 1},
    "CF": {"att_fill": 4, "tanh_done": 4, "out_ready": 1},
    "PREP": {},
    "FOLD": {"att_fill": 6},
    "CHECK": {"att_fill": 1, "check_low": 0, "check_sum": 0, "check_red": 1},
}
NOT_SEMAPHORES = {"ffn_fill", "att_fill", "a_tile"}


def steps_from(plan):
    steps = []
    for word in plan.split():
        who, _, name = word.rpartition(":")
        kind = "CL2" if name == "CL2" else name.rstrip("0123456789")
        digits = name[len(kind):]
        steps.append((kind, int(digits) if digits else 0, who))
    return steps


PLAN = steps_from("""
    c:CL U0 U1 U2 U3 G0 c:T G1 c:CV c:CZ G2 c:CS0 c:CS1 c:CP0 c:CS2 c:CP1 c:CS3 G3 c:CO0 c:CP2 H0 c:CO1 c:CP3
    H1 c:CO2 c:CO3 c:CL2 H2 BL1 H3 c:T BT1 a:AL W0 c:CF
    U0 a:T U1 a:AKV0 a:AKV1 U2 a:AKV2 a:AKV3 U3 a:AQ G0 G1 a:AS G2 a:AM G3 a:AO H0 n:BL0 H1 H2 H3 n:BT0 W1""")


def only(*whose):
    return [s for s in PLAN if s[2] in whose]


def with_checks(steps, behind):
    out, behind = [], dict(behind)
    for s in steps:
        out.append(s)
        if s[:2] in behind:
            out.append(("CHECK", behind.pop(s[:2]), ""))
    return out


CHECKED = ["w12", "h1", "h2", "w3"]


def total(steps):
    out = {}
    for s in steps:
        for name, n in adds(s).items():
            out[name] = out.get(name, 0) + n
    return out


def adds(step):
    more = dict(ADDS[step[0]])
    if step[0] == "CHECK":
        more["check_low"] = more["check_sum"] = CHECK_CHUNKS[step[1]]
    return more


CHECK_CHUNKS = [2 * KD * HID // CHUNK, KH * HID // CHUNK, KH * HID // CHUNK, KH * D // CHUNK]


class Counts:

    def __init__(self, start, rate=None, it=None):
        self.now, self.rate, self.it = dict(start), rate or {}, it
        self.seen = {}

    def value(self, name, k=0):
        v = self.now.get(name, 0) + k
        r = self.rate.get(name, 0)
        return v if self.it is None or not r else self.it * r + v

    def bank(self, ring, k):
        v = self.now.get(ring, 0) + k
        n, r = v // RING + 1, self.rate.get(ring, 0) // RING
        return v % RING, (n if self.it is None or not r else self.it * r + n)

    def ago(self, ring, kind, j):
        return self.seen[kind, j][ring] - self.now[ring]

    def ahead(self, step):
        self.seen[step[:2]] = dict(self.now)
        for name, n in adds(step).items():
            self.now[name] = self.now.get(name, 0) + n


def before(value):
    return None if isinstance(value, int) and value <= 1 else value - 1


PROLOGUE = steps_from("a:AL PREP a:T a:AKV0 a:AKV1 a:AKV2 a:AKV3 a:AQ a:AS a:AM a:AO n:BL0 n:BT0 FOLD CHECK0 CHECK1")
FIRST = with_checks(only("", "a", "n"), {("G", 1): 2, ("H", 1): 3})
BODY = PLAN
LAST = only("", "c")
TAIL = only("c")


def build(nc, a):
    with ExitStack() as ctx:
        def sb(name, shape, dt=F32):
            return ctx.enter_context(nc.sbuf_tensor(name, shape, dt))

        def sem(name):
            return ctx.enter_context(nc.semaphore(name))

        banks = {r: [ctx.enter_context(nc.psum_tensor(f"{r}_{b}", [P, 512], F32)) for b in range(RING)]
                 for r in ("ffn_fill", "att_fill")}

        w12 = sb("w12", [P, 2, KD, HID], F32R)
        h1 = sb("h1", [P, KH, HID], F32R)
        h2 = sb("h2", [P, KH, HID], F32R)
        w3 = sb("w3", [P, KH, D], F32R)
        checked = [w12[:].rearrange("p a k n -> p (a k n)"), h1[:].rearrange("p k n -> p (k n)"),
                   h2[:].rearrange("p k n -> p (k n)"), w3[:].rearrange("p k n -> p (k n)")]
        wq = sb("wq", [P, KD, D])
        wkv = sb("wkv", [P, KD, 2 * D])
        wo = sb("wo", [P, KD, D])
        wz = sb("wz", [P, KD, D])
        wvo = sb("wvo", [P, KD, D])
        wf = sb("wf", [P, KD, D])
        scales = sb("scales", [P, 4, KH])
        cols = sb("cols", [P, 4, KD])
        half_bq = sb("half_bq", [P, KD])
        z_bias = sb("z_bias", [P, KD + 1])
        rows = sb("rows", [P, 7, D])
        bv_row, bo_row, s3_row, bout_row, fb_row, vb_row, u_row = (rows[:, r, :] for r in range(7))
        ident = sb("ident", [P, P])
        ones = sb("ones", [P, P])
        head_mask = sb("head_mask", [P, P])

        x = sb("x", [P, SLOTS, NB, D])
        xn_b = sb("xn_b", [P, HB, D])
        xt_hi = sb("xt_hi", [P, KD, HT], F32R)
        xt_lo = sb("xt_lo", [P, KD, HT], F32R)
        act_hi = [sb(f"act{n}_hi", [P, KH, HT], F32R) for n in range(2)]
        act_lo = [sb(f"act{n}_lo", [P, KH, HT], F32R) for n in range(2)]
        gated = sb("gated", [P, 2, 2, HT])
        whole = sb("whole", [P, 3, 2, HT])
        w_tmp = xn_b
        xn_a = sb("xn_a", [P, NB, D])
        xn_c = sb("xn_c", [P, NB, D])
        xt = sb("xt", [P, KD, S])
        qz = sb("qz", [P, KD, S])
        kv_a = sb("kv_a", [P, NB, D])
        kv_b = sb("kv_b", [P, NB, D])
        prob = kv_b[:].rearrange("p (r a) d -> p r (a d)", r=2)
        prob_t = sb("prob_t", [P, 2, NB, P])
        kv = sb("kv", [P, KD, P])
        m_sb = sb("m_sb", [P, KD, D])
        st = sb("st", [P, NB, 6])
        xn_of = {"a": xn_a, "c": xn_c}
        mv = sb("mv", [P, NB, 2])
        var_eps = sb("var_eps", [P, NB])
        minus_half = sb("minus_half", [P, NB])
        rstd = sb("rstd", [P, NB])
        cq = sb("cq", [P, 2, NB])
        sm = sb("sm", [P, 5, NB])
        lowsum = sb("lowsum", [P, 16 + 2])
        flag = sb("flag", [P, 4])

        raw = [x[:, 1 + n // 2, 2 * (n % 2):2 * (n % 2) + 2, :] for n in range(6)]
        raw_q, raw_k, raw_v, raw_out, raw_f, raw_a1 = raw
        spare = whole[:].rearrange("p a b n -> p (a b n)")
        raw_a2 = spare[:, 0:512].rearrange("p (k n) -> p k n", k=KD)
        t1 = spare[:, 512:1024].rearrange("p (k n) -> p k n", k=KD)
        bk_wide = spare[:, 1024:1280].rearrange("p (k n) -> p k n", k=KD)
        bv_wide = spare[:, 1280:1536].rearrange("p (k n) -> p k n", k=KD)
        low = prob_t[:].rearrange("p r a b -> p r (a b)").bitcast(U32)
        squares = kv_b[:].rearrange("p a d -> p (a d)")

        full = {r: [sem(f"{r}_full{b}") for b in range(RING)] for r in banks}
        taken = {r: [sem(f"{r}_taken{b}") for b in range(RING)] for r in banks}
        names = sorted({n for added in ADDS.values() for n in added} - NOT_SEMAPHORES)
        s = {n: sem(n) for n in names}
        x_loaded, x_stored = sem("x_loaded"), sem("x_stored")
        a_loaded, c_loaded, small_loaded = sem("a_loaded"), sem("c_loaded"), sem("small_loaded")
        w_bounced = [sem(f"{n}_bounced") for n in CHECKED]
        w_loaded = [sem(f"{n}_loaded") for n in CHECKED]
        consts, wide = sem("consts"), sem("wide")

        start = {}
        phases = []
        for steps in (PROLOGUE, FIRST):
            phases.append(dict(start))
            for n, k in total(steps).items():
                start[n] = start.get(n, 0) + k
        phases.append(dict(start))
        rate = total(BODY)
        for n, k in rate.items():
            start[n] = start.get(n, 0) + k * (T - 2)
        phases.append(dict(start))
        for n, k in total(LAST).items():
            start[n] = start.get(n, 0) + k
        phases.append(dict(start))

        def walk(eng, part):
            def steps_of(steps, counts, slots):
                for step in steps:
                    part(step, counts, slots)
                    counts.ahead(step)

            steps_of(PROLOGUE, Counts(phases[0]), {"a": 0, "n": 0})
            steps_of(FIRST, Counts(phases[1]), {"": 0, "a": 1, "n": 1})
            with eng.Fori(0, T - 2) as it:
                steps_of(BODY, Counts(phases[2], rate, it),
                         {"c": eng.snap(it % SLOTS), "": eng.snap((it + 1) % SLOTS),
                          "a": eng.snap((it + 2) % SLOTS), "n": eng.snap((it + 2) % SLOTS)})
            steps_of(LAST, Counts(phases[3]), {"c": (T - 2) % SLOTS, "": (T - 1) % SLOTS})
            steps_of(TAIL, Counts(phases[4]), {"c": (T - 1) % SLOTS})

        def wait(eng, which, value):
            if value is not None and not (isinstance(value, int) and value <= 0):
                eng.wait_ge(which, value)

        def wait_apart(eng, which, value):
            if isinstance(value, int):
                eng.wait_ge(which, value)
            else:
                register = eng.to_reg(value)
                eng.wait_ge(consts, 7)
                eng.wait_ge(which, register)

        def to_fill(eng, c, ring, k):
            b, n = c.bank(ring, k)
            wait(eng, taken[ring][b], before(n))
            return banks[ring][b], full[ring][b]

        def filled(eng, c, ring, k):
            b, n = c.bank(ring, k)
            eng.wait_ge(full[ring][b], n)
            return banks[ring][b], taken[ring][b]

        def wait_taken(eng, c, ring, k):
            b, n = c.bank(ring, k)
            eng.wait_ge(taken[ring][b], n)

        two = lambda bank: bank[:].rearrange("p (a n) -> p a n", a=2)
        four = lambda bank: bank[:].rearrange("p (a n) -> p a n", a=4)
        row2 = lambda row: row[:, None, :].broadcast_to([P, 2, D])

        block = ctx.enter_context(nc.Block())

        x_in = a["L0_attn_x"].rearrange("t (b p) d -> t p b d", p=P)
        x_out = a["out"].rearrange("t (b p) d -> t p b d", p=P)

        def km(name):
            return a[name].rearrange("(k p) n -> p k n", p=P)

        @block.sync
        def _(sp):
            sp.dma_start(x[:, 0], x_in[0]).then_inc(x_loaded, 16)
            sp.dma_start(wkv[:, :, 0:D], km("wk0T")).then_inc(a_loaded, 16)
            sp.dma_start(wkv[:, :, D:2 * D], km("wv0T")).then_inc(a_loaded, 16)
            sp.dma_start(wq[:], km("wq0T")).then_inc(a_loaded, 16)
            sp.dma_start(wo[:], km("wo0T")).then_inc(a_loaded, 16)
            for n, name in enumerate(("bq0", "b_q", "b_k", "b_v")):
                sp.dma_start(cols[:, n, :], a[name]).then_inc(small_loaded, 16)
            for n, name in enumerate(("s1", "s2", "s_h1", "s_h2")):
                sp.dma_start(scales[:, n, :], a[name]).then_inc(small_loaded, 16)
            for n, name in enumerate(("L0_attn_bv", "L0_attn_bo", "L0_ffn_w3_s", "L1_attn_b_out", "L1_ffn_bias")):
                sp.dma_start(rows[:, n, :], a[name].rearrange("(o n) -> o n", o=1).broadcast_to([P, D]))\
                  .then_inc(small_loaded, 16)
            parts = [[("w1T", w12[:, 0]), ("w2T", w12[:, 1])], [("h1T", h1[:])], [("h2T", h2[:])], [("w3T", w3[:])]]

            def bounce(layer):
                for name, _ in parts[layer]:
                    sp.dma_start(a["scratch_" + name], a[name]).then_inc(w_bounced[layer], 16)

            def land(layer):
                sp.wait_ge(w_bounced[layer], 16 * len(parts[layer]))
                for name, tile in parts[layer]:
                    sp.dma_start(tile.bitcast(F32), a["scratch_" + name].rearrange("(k p) n -> p k n", p=P))\
                      .then_inc(w_loaded[layer], 16)

            bounce(0)
            for tile, name in ((raw_q, "L1_attn_w_q"), (raw_k, "L1_attn_w_k"), (raw_v, "L1_attn_w_v"),
                               (raw_out, "woutT"), (raw_f, "wfT"), (raw_a1, "L1_ffn_aux_weight1"),
                               (raw_a2, "L1_ffn_aux_weight2")):
                sp.dma_start(tile, km(name)).then_inc(c_loaded, 16)
            bounce(1)
            land(0)
            bounce(2)
            land(1)
            bounce(3)
            land(2)
            land(3)
            c = Counts(phases[0])
            for step in PROLOGUE:
                if step[0] == "FOLD":
                    wait_taken(sp, c, "att_fill", 5)
                c.ahead(step)
            for t in range(1, SLOTS):
                sp.dma_start(x[:, t], x_in[t]).then_inc(x_loaded, 16)
                sp.wait_ge(x_loaded, 16 * (t + 1))
            with sp.Fori(0, T - SLOTS) as t:
                slot = sp.snap(t % SLOTS)
                sp.wait_ge(s["out_ready"], t + 1)
                sp.dma_start(x_out[t], x[:, slot]).then_inc(x_stored, 16)
                wait_apart(sp, x_stored, 16 * t + 16)
                wait_apart(sp, x_loaded, 16 * t + 16 * SLOTS)
                sp.dma_start(x[:, slot], x_in[t + SLOTS]).then_inc(x_loaded, 16)
            for t in range(T - SLOTS, T):
                sp.wait_ge(s["out_ready"], t + 1)
                sp.dma_start(x_out[t], x[:, t % SLOTS]).then_inc(x_stored, 16)
            sp.wait_ge(x_stored, 16 * T)

        @block.gpsimd
        def _(pool):
            pool.memset(ident[:], 0.0).then_inc(consts, 1)
            pool.memset(head_mask[:], 1.0).then_inc(consts, 1)
            pool.memset(ones[:], 1.0).then_inc(consts, 1)
            pool.memset(minus_half[:], -0.5).then_inc(consts, 1)
            pool.wait_ge(consts, 4)
            pool.affine_select(out=ident[:], in_=ident[:], compare_op=ALU.not_equal, fill=1.0, base=0,
                               pattern=[[-1, P]], channel_multiplier=1).then_inc(consts, 1)
            hm = head_mask[:].rearrange("p (g r) -> p g r", r=HEAD)
            pool.affine_select(out=hm, in_=hm, compare_op=ALU.is_ge, fill=0.0, base=0,
                               pattern=[[-HEAD, P // HEAD], [0, HEAD]], channel_multiplier=1).then_inc(consts, 1)
            pool.wait_ge(consts, 6)
            pool.affine_select(out=hm, in_=hm, compare_op=ALU.is_ge, fill=0.0, base=HEAD - 1,
                               pattern=[[HEAD, P // HEAD], [0, HEAD]], channel_multiplier=-1).then_inc(consts, 1)

            def add_bias(c, xs, bias_row):
                pool.wait_ge(small_loaded, 16 * 13)
                wait_apart(pool, s["xn_ready"], c.value("xn_ready", 1))
                for b in range(0, NB, 2):
                    last = pool.tensor_tensor(xs[:, b:b + 2, :], xs[:, b:b + 2, :], row2(bias_row), ALU.add)
                last.then_inc(s["bias_added"], 1)

            def inverse_deviation(c, nb):
                wait_apart(pool, s["ln_stats"], c.value("ln_stats", 3))
                pool.tensor_tensor(rstd[:, :nb], var_eps[:, :nb], minus_half[:, :nb], ALU.pow)\
                    .then_inc(s["ln_pow"], 1)

            def part(step, c, slots):
                kind, j, who = step
                if kind in ("AL", "CL", "CL2", "BL"):
                    inverse_deviation(c, HB if kind == "BL" else NB)
                    if kind in ("AL", "CL"):
                        add_bias(c, x[:, slots[who]], bo_row if kind == "AL" else bout_row)
                elif kind == "U":
                    n = c.now.get("ffn_ready", 0)
                    pool.wait_ge(s["hi_ready"], c.value("hi_ready", 1))
                    blocks = slice(2 * j, 2 * j + 2)
                    pool.tensor_tensor(act_lo[0][:, blocks], whole[:, n % 3], act_hi[0][:, blocks].bitcast(F32),
                                       ALU.subtract).then_inc(s["ffn_ready"], 1)
                elif kind == "CF":
                    for b in range(NB):
                        wait_apart(pool, s["tanh_done"], c.value("tanh_done", b + 1))
                        xb = x[:, slots[who], b, :]
                        last = pool.tensor_tensor(xb, xb, xn_c[:, b, :], ALU.add)
                    last.then_inc(s["out_ready"], 1)

            walk(pool, part)

        @block.vector
        def _(dve):
            def layernorm(c, xs, xn, nb):
                for b in range(nb):
                    last = dve.bn_stats(st[:, b, :], xs[:, b, :])
                last.then_inc(s["ln_stats"], 1)
                wait_apart(dve, s["ln_stats"], c.value("ln_stats", 1))
                for b in range(nb):
                    last = dve.bn_aggr(mv[:, b, :], st[:, b, :])
                last.then_inc(s["ln_stats"], 1)
                dve.wait_ge(s["ln_stats"], c.value("ln_stats", 2))
                dve.tensor_scalar(var_eps[:, :nb], mv[:, :nb, 1], EPS, None, ALU.add).then_inc(s["ln_stats"], 1)
                dve.wait_ge(s["ln_pow"], c.value("ln_pow", 1))
                for b in range(nb):
                    last = dve.tensor_scalar(xn[:, b, :], xs[:, b, :], mv[:, b, 0:1], rstd[:, b:b + 1],
                                             ALU.subtract, ALU.mult)
                last.then_inc(s["xn_ready"], 1)

            def part(step, c, slots):
                kind, j, who = step
                if kind == "AL":
                    wait_apart(dve, x_loaded, c.value("a_tile", 1) * 16)
                    layernorm(c, x[:, slots[who]], xn_a, NB)
                elif kind == "CL":
                    wait_apart(dve, s["b_done"], c.value("b_done"))
                    layernorm(c, x[:, slots[who]], xn_c, NB)
                    dve.wait_ge(s["xn_ready"], c.value("xn_ready", 1))
                    for b in range(NB):
                        last = dve.tensor_tensor_reduce(kv_a[:, b, :], xn_c[:, b, :], u_row, 1.0, 0.0,
                                                        ALU.mult, ALU.add, cq[:, 0, b:b + 1])
                    last.then_inc(s["key_bias"], 1)
                    dve.wait_ge(s["key_bias"], c.value("key_bias", 1))
                    dve.tensor_scalar(cq[:, 1, :], cq[:, 0, :], z_bias[:, KD:KD + 1], None, ALU.add)\
                       .then_inc(s["key_bias"], 1)
                elif kind == "CL2":
                    b, n = c.bank("att_fill", -1)
                    wait_apart(dve, taken["att_fill"][b], n)
                    layernorm(c, x[:, slots[who]], xn_c, NB)
                elif kind == "BL":
                    xs = x[:, slots[who]]
                    if j == 0:
                        b, n = c.bank("att_fill", -1)
                        wait_apart(dve, taken["att_fill"][b], n)
                    layernorm(c, xs[:, HB * j:HB * j + HB], xn_b, HB)
                elif kind == "T":
                    bank, out = filled(dve, c, "att_fill", 1)
                    dve.tensor_copy(xt[:, 1, :], bank[:]).then_inc(out, 1)
                elif kind == "BT":
                    bank, out = filled(dve, c, "ffn_fill", 0)
                    dve.wait_ge(s["bt_hi"], c.value("bt_hi", 1))
                    dve.tensor_tensor(xt_lo[:], two(bank), xt_hi[:].bitcast(F32), ALU.subtract).then_inc(out, 1)
                elif kind == "U":
                    n = c.now.get("ffn_ready", 0)
                    wait_taken(dve, c, "ffn_fill", 0)
                    bank, out = filled(dve, c, "ffn_fill", 1)
                    wait(dve, s["ffn_ready"], c.value("ffn_ready", -2))
                    for o in range(2):
                        last = dve.scalar_tensor_tensor(whole[:, n % 3, o, :], two(bank)[:, o, :],
                                                        scales[:, 1, 2 * j + o:2 * j + o + 1],
                                                        gated[:, j % 2, o, :], ALU.mult, ALU.mult)
                    last.then_inc(out, 1)
                    wait_taken(dve, c, "ffn_fill", 1)
                    dve.tensor_copy(act_hi[0][:, 2 * j:2 * j + 2], whole[:, n % 3]).then_inc(s["hi_ready"], 1)
                elif kind in ("G", "H"):
                    n, dst, blocks = c.now.get("ffn_ready", 0), 1 if kind == "G" else 0, slice(2 * j, 2 * j + 2)
                    wait_taken(dve, c, "ffn_fill", 0)
                    dve.tensor_copy(act_hi[dst][:, blocks], whole[:, n % 3]).then_inc(s["hi_ready"], 1)
                    dve.wait_ge(s["hi_ready"], c.value("hi_ready", 1))
                    dve.tensor_tensor(act_lo[dst][:, blocks], whole[:, n % 3], act_hi[dst][:, blocks].bitcast(F32),
                                      ALU.subtract).then_inc(s["ffn_ready"], 1)
                elif kind == "W":
                    bank, out = filled(dve, c, "ffn_fill", 0)
                    dve.tensor_tensor(w_tmp[:], two(bank), row2(s3_row), ALU.mult).then_inc(out, 1)
                    wait_taken(dve, c, "ffn_fill", 0)
                    xs = x[:, slots[who], HB * j:HB * j + HB, :]
                    dve.tensor_tensor(xs, xs, w_tmp[:], ALU.add).then_inc(s["b_done"], 1)
                elif kind == "AKV":
                    dve.wait_ge(s["k_silu"], c.value("k_silu", 1))
                    bank, out = filled(dve, c, "att_fill", 0)
                    dve.tensor_tensor(kv_b[:, j, :], bank[:, D:2 * D], bv_row, ALU.add).then_inc(out, 1)
                    dve.tensor_scalar(kv_a[:, j, :], kv_a[:, j, :], 1.0, None, ALU.add).then_inc(s["phik_ready"], 1)
                elif kind == "AQ":
                    for k in range(KD):
                        wait_taken(dve, c, "att_fill", k)
                        dve.tensor_scalar(qz[:, k, :], qz[:, k, :], 1.0, None, ALU.add).then_inc(s["phiq_ready"], 1)
                elif kind == "AS":
                    bank, out = filled(dve, c, "att_fill", 0)
                    dve.tensor_tensor(kv[:], four(bank)[:, 0:2, :], head_mask[:, None, :].broadcast_to([P, 2, P]),
                                      ALU.mult).then_inc(out, 1)
                elif kind == "AO":
                    dve.wait_ge(s["bias_added"], c.value("bias_added"))
                    for g in range(2):
                        bank, out = filled(dve, c, "att_fill", g)
                        xs = x[:, slots[who], 2 * g:2 * g + 2, :]
                        dve.tensor_tensor(xs, two(bank), xs, ALU.add).then_inc(out, 1)
                elif kind == "CV":
                    for g in range(2):
                        bank, out = filled(dve, c, "att_fill", g)
                        dve.tensor_tensor(kv_a[:, 2 * g:2 * g + 2, :], two(bank), row2(vb_row), ALU.add).then_inc(out, 1)
                elif kind == "CS":
                    bank, _ = filled(dve, c, "att_fill", 0)
                    q = slice(j, j + 1)
                    dve.tensor_reduce(sm[:, 0, q], bank[:], AX.X, ALU.max).then_inc(s["row_max"], 1)
                    dve.wait_ge(s["row_max"], c.value("row_max", 1))
                    dve.scalar_tensor_tensor(sm[:, 1, q], sm[:, 0, q], cq[:, 1, q], cq[:, 1, q],
                                             ALU.add, ALU.subtract).then_inc(s["row_max"], 1)
                    dve.wait_ge(s["row_max"], c.value("row_max", 2))
                    dve.tensor_scalar(sm[:, 2, q], sm[:, 1, q], -float(D) ** -0.5, None, ALU.mult)\
                       .then_inc(s["exp_bias"], 1)
                elif kind == "CO":
                    q = slice(j, j + 1)
                    bank, out = filled(dve, c, "att_fill", 0)
                    dve.reciprocal(sm[:, 4, q], sm[:, 3, q]).then_inc(s["inverse"], 1)
                    dve.wait_ge(s["inverse"], c.value("inverse", 1))
                    dve.wait_ge(s["bias_added"], c.value("bias_added"))
                    xs = x[:, slots[who], j, :]
                    dve.scalar_tensor_tensor(xs, bank[:, 0:D], sm[:, 4, q], xs, ALU.mult, ALU.add).then_inc(out, 1)
                elif kind == "CF":
                    for b in range(NB):
                        bank, out = filled(dve, c, "att_fill", b)
                        dve.tensor_tensor(xn_c[:, b, :], bank[:, 0:D], fb_row, ALU.add).then_inc(out, 1)
                elif kind == "PREP":
                    dve.wait_ge(small_loaded, 16 * 13)
                    dve.wait_ge(consts, 7)
                    dve.tensor_scalar(half_bq[:], cols[:, 0, :], 0.5, None, ALU.mult).then_inc(wide, 1)
                elif kind == "FOLD":
                    for k in range(KD):
                        dve.tensor_scalar(bk_wide[:, k, :], ones[:], cols[:, 2, k:k + 1], None, ALU.mult)\
                           .then_inc(wide, 1)
                        dve.tensor_scalar(bv_wide[:, k, :], ones[:], cols[:, 3, k:k + 1], None, ALU.mult)\
                           .then_inc(wide, 1)
                    for n, dst in enumerate((t1, wz[:], wvo[:])):
                        bank, out = filled(dve, c, "att_fill", n)
                        dve.tensor_copy(dst, two(bank)).then_inc(out, 1)
                    bank, out = filled(dve, c, "att_fill", 3)
                    dve.tensor_copy(z_bias[:], bank[:, 0:KD + 1]).then_inc(out, 1)
                    bank, out = filled(dve, c, "att_fill", 4)
                    dve.tensor_copy(rows[:, 5:7, :], two(bank)).then_inc(out, 1)
                    bank, out = filled(dve, c, "att_fill", 5)
                    dve.tensor_copy(wf[:], two(bank)).then_inc(out, 1)
                elif kind == "CHECK":
                    chunks = CHECK_CHUNKS[j]
                    dve.wait_ge(w_loaded[j], 16 * (2 if j == 0 else 1))
                    words = checked[j].bitcast(U32)
                    done = c.now.get("check_low", 0)

                    def low_bits(n, r):
                        dve.tensor_scalar(low[:, r, :], words[:, bass.ds(n * (2 * CHUNK) + r * CHUNK, CHUNK)],
                                          LOWBITS, None, ALU.bitwise_and).then_inc(s["check_low"], 1)

                    for r in range(2):
                        low_bits(0, r)
                    with dve.Fori(1, chunks // 2) as n:
                        for r in range(2):
                            dve.wait_ge(s["check_sum"], n * 2 + (done + r - 1))
                            low_bits(n, r)
                    dve.wait_ge(s["check_sum"], c.value("check_sum", chunks))
                    dve.tensor_reduce(lowsum[:, 16:17], lowsum[:, 0:chunks], AX.X, ALU.add).then_inc(s["check_red"], 1)
                    bank, out = filled(dve, c, "att_fill", 0)
                    dve.tensor_copy(flag[:, j:j + 1], bank[:, 0:1]).then_inc(out, 1)

            walk(dve, part)

        @block.scalar
        def _(act):
            def part(step, c, slots):
                kind, j, who = step
                if kind == "T":
                    bank, out = filled(act, c, "att_fill", 0)
                    act.activation(xt[:, 0, :], bank[:], ACT.Copy).then_inc(out, 1)
                elif kind == "BT":
                    bank, _ = filled(act, c, "ffn_fill", 0)
                    act.activation(xt_hi[:], two(bank), ACT.Copy).then_inc(s["bt_hi"], 1)
                elif kind == "U":
                    if j >= 2:
                        wait_taken(act, c, "ffn_fill", -3)
                    bank, out = filled(act, c, "ffn_fill", 0)
                    for o in range(2):
                        last = act.activation(gated[:, j % 2, o, :], two(bank)[:, o, :], ACT.Silu,
                                              scale=scales[:, 0, 2 * j + o:2 * j + o + 1])
                    last.then_inc(out, 1)
                elif kind in ("G", "H"):
                    n = c.now.get("ffn_ready", 0)
                    act.wait_ge(s["ffn_ready"], c.value("ffn_ready", -2))
                    bank, out = filled(act, c, "ffn_fill", 0)
                    layer = 2 if kind == "G" else 3
                    for o in range(2):
                        last = act.activation(whole[:, n % 3, o, :], two(bank)[:, o, :], ACT.Gelu,
                                              scale=scales[:, layer, 2 * j + o:2 * j + o + 1])
                    last.then_inc(out, 1)
                elif kind == "AKV":
                    bank, _ = filled(act, c, "att_fill", 0)
                    act.activation(kv_a[:, j, :], bank[:, 0:D], ACT.Silu, scale=HEAD ** -0.25)\
                       .then_inc(s["k_silu"], 1)
                elif kind == "AQ":
                    act.wait_ge(wide, 1)
                    for k in range(KD):
                        bank, out = filled(act, c, "att_fill", k)
                        act.activation(qz[:, k, :], bank[:], ACT.Silu, bias=half_bq[:, k:k + 1],
                                       scale=HEAD ** -0.25).then_inc(out, 1)
                elif kind == "AM":
                    bank, out = filled(act, c, "att_fill", 0)
                    act.activation(m_sb[:], two(bank), ACT.Copy).then_inc(out, 1)
                elif kind == "CZ":
                    for k in range(KD):
                        bank, out = filled(act, c, "att_fill", k)
                        act.activation(qz[:, k, :], bank[:], ACT.Identity, bias=z_bias[:, k:k + 1]).then_inc(out, 1)
                elif kind == "CS":
                    bank, out = filled(act, c, "att_fill", 0)
                    act.wait_ge(s["exp_bias"], c.value("exp_bias", 1))
                    q = slice(j, j + 1)
                    act.activation(prob[:, j % 2, :], bank[:], ACT.Exp, bias=sm[:, 2, q], scale=float(D) ** -0.5,
                                   accum_out=sm[:, 3, q]).then_inc(out, 1)
                elif kind == "CP":
                    bank, out = filled(act, c, "att_fill", 0)
                    act.activation(prob_t[:, j % 2], four(bank), ACT.Copy).then_inc(out, 1)
                elif kind == "CF":
                    for b in range(NB):
                        wait_taken(act, c, "att_fill", b)
                        act.activation(xn_c[:, b, :], xn_c[:, b, :], ACT.Tanh).then_inc(s["tanh_done"], 1)
                elif kind == "CHECK":
                    done = c.now.get("check_low", 0)
                    with act.Fori(0, CHECK_CHUNKS[j] // 2) as n:
                        for r in range(2):
                            act.wait_ge(s["check_low"], n * 2 + (done + r + 1))
                            act.activation(squares[:, r * CHUNK:(r + 1) * CHUNK], low[:, r, :], ACT.Square,
                                           accum_out=lowsum[:, bass.ds(n * 2 + r, 1)]).then_inc(s["check_sum"], 1)

            walk(act, part)

        @block.tensor
        def _(pe):
            flags = {}

            def product(out, pairs):
                for n, (lhsT, rhs) in enumerate(pairs):
                    last = pe.matmul(out, lhsT, rhs, start=n == 0, stop=n == len(pairs) - 1)
                return last

            def ffn_products(layer, emit):
                with pe.If(flags[layer] != 0):
                    emit(lambda ap: ap.bitcast(F32))
                with pe.Else():
                    emit(lambda ap: ap)

            def hidden(c, layer, weights, src, j):
                bank, done = to_fill(pe, c, "ffn_fill", 0)

                def emit(view):
                    for k in range(KH):
                        if j == 0 and k % 2 == 0:
                            pe.wait_ge(s["ffn_ready"], c.value("ffn_ready", k // 2 + 1 - PAIRS))
                        for o in range(2):
                            w = weights[:, k, (2 * j + o) * P:(2 * j + o + 1) * P]
                            for half, moving in enumerate((act_hi[src], act_lo[src])):
                                last = pe.matmul(two(bank)[:, o, :], view(w), view(moving[:, k, :]),
                                                 start=k == 0 and o == 0 and half == 0,
                                                 stop=k == KH - 1 and half == 1, skip_group_check=True)
                    last.then_inc(done, 1)

                ffn_products(layer, emit)

            def part(step, c, slots):
                kind, j, who = step
                if kind == "T":
                    pe.wait_ge(s["xn_ready"], c.value("xn_ready"))
                    for k in range(KD):
                        bank, done = to_fill(pe, c, "att_fill", k)
                        for b in range(NB):
                            last = pe.transpose(four(bank)[:, b, :], xn_of[who][:, b, k * P:(k + 1) * P], ident[:])
                        last.then_inc(done, 1)
                elif kind == "BT":
                    pe.wait_ge(s["xn_ready"], c.value("xn_ready"))
                    bank, done = to_fill(pe, c, "ffn_fill", 0)
                    for k in range(KD):
                        for b in range(HB):
                            last = pe.transpose(two(bank)[:, k, b * P:(b + 1) * P],
                                                xn_b[:, b, k * P:(k + 1) * P], ident[:])
                    last.then_inc(done, 1)
                elif kind == "U":
                    if j == 0:
                        wait_taken(pe, c, "ffn_fill", -1 if c.it is None and c.now["ffn_fill"] == 1 else -2)
                    a_bank, a_done = to_fill(pe, c, "ffn_fill", 0)
                    b_bank, b_done = to_fill(pe, c, "ffn_fill", 1)

                    def emit(view):
                        for which, (bank, done) in enumerate(((a_bank, a_done), (b_bank, b_done))):
                            for o in range(2):
                                cols_o = slice((2 * j + o) * P, (2 * j + o + 1) * P)
                                last = product(two(bank)[:, o, :],
                                               [(view(w12[:, which, k, cols_o]), view(moving[:, k, :]))
                                                for k in range(KD) for moving in (xt_hi, xt_lo)])
                            last.then_inc(done, 1)

                    ffn_products(0, emit)
                elif kind == "G":
                    hidden(c, 1, h1, 0, j)
                elif kind == "H":
                    hidden(c, 2, h2, 1, j)
                elif kind == "W":
                    bank, done = to_fill(pe, c, "ffn_fill", 0)

                    def emit(view):
                        for k in range(KH):
                            if k % 2 == 0:
                                pe.wait_ge(s["ffn_ready"], c.value("ffn_ready", k // 2 + 1 - PAIRS))
                            for b in range(HB):
                                for half, part_of in enumerate((act_hi[0], act_lo[0])):
                                    last = pe.matmul(two(bank)[:, b, :], view(part_of[:, k, b * P:(b + 1) * P]),
                                                     view(w3[:, k, :]), start=k == 0 and b == 0 and half == 0,
                                                     stop=k == KH - 1 and half == 1, skip_group_check=True)
                        last.then_inc(done, 1)

                    ffn_products(3, emit)
                elif kind == "AKV":
                    if j == 0:
                        for k in range(KD):
                            wait_taken(pe, c, "att_fill", k - 2)
                        if c.it is None:
                            pe.wait_ge(a_loaded, 16 * 4)
                    bank, done = to_fill(pe, c, "att_fill", 0)
                    product(bank[:], [(xt[:, k, j * P:(j + 1) * P], wkv[:, k, :]) for k in range(KD)])\
                        .then_inc(done, 1)
                elif kind == "AQ":
                    for o in range(KD):
                        bank, done = to_fill(pe, c, "att_fill", o)
                        product(bank[:], [(wq[:, k, o * P:(o + 1) * P], xt[:, k, :]) for k in range(KD)])\
                            .then_inc(done, 1)
                elif kind == "AS":
                    pe.wait_ge(s["phik_ready"], c.value("phik_ready"))
                    bank, done = to_fill(pe, c, "att_fill", 0)
                    for g in range(KD):
                        cols_g = slice(g * P, (g + 1) * P)
                        last = product(four(bank)[:, g, :],
                                       [(kv_b[:, b, cols_g], kv_a[:, b, cols_g]) for b in range(NB)])
                    last.then_inc(done, 1)
                elif kind == "AM":
                    wait_taken(pe, c, "att_fill", -1)
                    bank, done = to_fill(pe, c, "att_fill", 0)
                    for g in range(KD):
                        last = product(two(bank)[:, g, :], [(kv[:, g, :], wo[:, g, :])])
                    last.then_inc(done, 1)
                elif kind == "AO":
                    wait_taken(pe, c, "att_fill", -1)
                    pe.wait_ge(s["phiq_ready"], c.value("phiq_ready"))
                    for g in range(2):
                        bank, done = to_fill(pe, c, "att_fill", g)
                        for b in range(2):
                            tok = slice((2 * g + b) * P, (2 * g + b + 1) * P)
                            last = product(two(bank)[:, b, :], [(qz[:, k, tok], m_sb[:, k, :]) for k in range(KD)])
                        last.then_inc(done, 1)
                elif kind == "CV":
                    for k in range(KD):
                        wait_taken(pe, c, "att_fill", c.ago("att_fill", "T", 0) + k)
                    for g in range(2):
                        bank, done = to_fill(pe, c, "att_fill", g)
                        for b in range(2):
                            tok = slice((2 * g + b) * P, (2 * g + b + 1) * P)
                            last = product(two(bank)[:, b, :], [(xt[:, k, tok], wvo[:, k, :]) for k in range(KD)])
                        last.then_inc(done, 1)
                elif kind == "CZ":
                    for o in range(KD):
                        bank, done = to_fill(pe, c, "att_fill", o)
                        product(bank[:], [(wz[:, k, o * P:(o + 1) * P], xt[:, k, :]) for k in range(KD)])\
                            .then_inc(done, 1)
                elif kind == "CS":
                    if j == 0:
                        for k in range(KD):
                            wait_taken(pe, c, "att_fill", c.ago("att_fill", "CZ", 0) + k)
                    bank, done = to_fill(pe, c, "att_fill", 0)
                    product(bank[:], [(qz[:, k, j * P:(j + 1) * P], xt[:, k, :]) for k in range(KD)])\
                        .then_inc(done, 1)
                elif kind == "CP":
                    wait_taken(pe, c, "att_fill", c.ago("att_fill", "CS", j))
                    bank, done = to_fill(pe, c, "att_fill", 0)
                    for b in range(NB):
                        last = pe.transpose(four(bank)[:, b, :], prob[:, j % 2, b * P:(b + 1) * P], ident[:])
                    last.then_inc(done, 1)
                elif kind == "CO":
                    if j == 0:
                        for g in range(2):
                            wait_taken(pe, c, "att_fill", c.ago("att_fill", "CV", 0) + g)
                    wait_taken(pe, c, "att_fill", c.ago("att_fill", "CP", j))
                    bank, done = to_fill(pe, c, "att_fill", 0)
                    product(bank[:, 0:D], [(prob_t[:, j % 2, b, :], kv_a[:, b, :]) for b in range(NB)])\
                        .then_inc(done, 1)
                elif kind == "CF":
                    for k in range(KD):
                        wait_taken(pe, c, "att_fill", c.ago("att_fill", "T", 0) + k)
                    for b in range(NB):
                        bank, done = to_fill(pe, c, "att_fill", b)
                        product(bank[:, 0:D], [(xt[:, k, b * P:(b + 1) * P], wf[:, k, :]) for k in range(KD)])\
                            .then_inc(done, 1)
                elif kind == "FOLD":
                    pe.wait_ge(c_loaded, 16 * 7)
                    pe.wait_ge(wide, 5)
                    blk = lambda o: slice(o * P, (o + 1) * P)
                    for n, (left, right) in enumerate(((raw_a1, raw_f), (raw_q, raw_k), (raw_v, raw_out))):
                        bank, done = to_fill(pe, c, "att_fill", n)
                        for o in range(KD):
                            last = product(two(bank)[:, o, :], [(left[:, k, blk(o)], right[:, k, :]) for k in range(KD)])
                        last.then_inc(done, 1)
                    bank, done = to_fill(pe, c, "att_fill", 3)
                    for o in range(KD):
                        product(bank[:, o:o + 1], [(raw_k[:, k, blk(o)], cols[:, 1, k:k + 1]) for k in range(KD)])
                    product(bank[:, KD:KD + 1], [(bk_wide[:, k, :], cols[:, 1, k:k + 1]) for k in range(KD)])\
                        .then_inc(done, 1)
                    bank, done = to_fill(pe, c, "att_fill", 4)
                    product(two(bank)[:, 0, :], [(bv_wide[:, k, :], raw_out[:, k, :]) for k in range(KD)])
                    product(two(bank)[:, 1, :], [(bk_wide[:, k, :], raw_q[:, k, :]) for k in range(KD)])\
                        .then_inc(done, 1)
                    wait_taken(pe, c, "att_fill", 0)
                    bank, done = to_fill(pe, c, "att_fill", 5)
                    for o in range(KD):
                        last = product(two(bank)[:, o, :], [(t1[:, k, blk(o)], raw_a2[:, k, :]) for k in range(KD)])
                    last.then_inc(done, 1)
                elif kind == "CHECK":
                    pe.wait_ge(s["check_red"], c.value("check_red", 1))
                    bank, done = to_fill(pe, c, "att_fill", 0)
                    product(bank[:, 0:1], [(ones[:], lowsum[:, 16:17])]).then_inc(done, 1)
                    wait_taken(pe, c, "att_fill", 0)
                    flags[j] = pe.value_load(flag[0:1, j:j + 1].bitcast(I32))

            pe.wait_ge(consts, 7)
            walk(pe, part)


def kernel(**inputs):
    import concourse.bacc as bacc
    from concourse.bass_utils import run_bass_kernel_spmd

    def t(name):
        return np.ascontiguousarray(np.asarray(inputs[name]).T)

    def columns(name):
        return np.ascontiguousarray(np.asarray(inputs[name]).reshape(-1, P).T)

    given = {
        "wq0T": t("L0_attn_Wq"), "wk0T": t("L0_attn_Wk"), "wv0T": t("L0_attn_Wv"), "wo0T": t("L0_attn_Wo"),
        "bq0": columns("L0_attn_bq"), "b_q": columns("L1_attn_b_q"), "b_k": columns("L1_attn_b_k"),
        "b_v": columns("L1_attn_b_v"), "s1": columns("L0_ffn_w1_s"), "s2": columns("L0_ffn_w2_s"),
        "s_h1": columns("L0_ffn_h1_s"), "s_h2": columns("L0_ffn_h2_s"),
        "w1T": t("L0_ffn_w1_w"), "w2T": t("L0_ffn_w2_w"), "h1T": t("L0_ffn_h1_w"), "h2T": t("L0_ffn_h2_w"),
        "w3T": t("L0_ffn_w3_w"), "woutT": t("L1_attn_w_out"), "wfT": t("L1_ffn_weight"),
    }
    for name in ("L0_attn_x", "L0_attn_bv", "L0_attn_bo", "L0_ffn_w3_s", "L1_attn_w_q", "L1_attn_w_k",
                 "L1_attn_w_v", "L1_attn_b_out", "L1_ffn_aux_weight1", "L1_ffn_aux_weight2", "L1_ffn_bias"):
        given[name] = np.ascontiguousarray(inputs[name])
    nc = bacc.Bacc("TRN2", target_bir_lowering=False, num_devices=1)
    arrays, args = {}, {}
    for name, array in given.items():
        arrays["in_" + name] = array
        args[name] = nc.dram_tensor("in_" + name, array.shape, F32, kind="ExternalInput").ap()
    for name in ("w1T", "w2T", "h1T", "h2T", "w3T"):
        args["scratch_" + name] = nc.dram_tensor("scratch_" + name, given[name].shape, F32, kind="Internal").ap()
    args["out"] = nc.dram_tensor("out_0", (T, S, D), F32, kind="ExternalOutput").ap()
    build(nc, args)
    r = run_bass_kernel_spmd(nc, [arrays], core_ids=[0])
    return r.results[0]["out_0"]
```

```python
from contextlib import ExitStack

import numpy as np
import concourse.bass as bass
from concourse import mybir

F32 = mybir.dt.float32
F32R = mybir.dt.float32r
U16 = mybir.dt.uint16
I32 = mybir.dt.int32
ALU = mybir.AluOpType
ACT = mybir.ActivationFunctionType
AX = mybir.AxisListType

P = 128
D = 256
KD = D // P
HID = 1024
KH = HID // P
S = 512
NB = S // P
T = 16
HEAD = 16
HT = S // 2
HB = HT // P
PAIRS = KH // 2
SLOTS = 4
WHOLES = 2
RING = 4
EPS = 1e-5
LOOK = 2048
SQUARED = 768

STATS = {"ln_stats": 3, "ln_pow": 1}
ADDS = {
    "U": {"ffn_fill": 2, "hi_ready": 1, "ffn_ready": 1},
    "G": {"ffn_fill": 1, "hi_ready": 1, "ffn_ready": 1},
    "H": {"ffn_fill": 1, "hi_ready": 1, "ffn_ready": 1},
    "W": {"ffn_fill": 1, "b_done": 1},
    "BST": STATS,
    "BNO": {"xn_ready": HB},
    "BT": {"ffn_fill": 1, "bt_hi": 1},
    "AST": {**STATS, "a_tile": 1},
    "ANO": {"xn_ready": NB},
    "AB": {"bias_added": 1},
    "CST": STATS,
    "CNO": {"xn_ready": NB},
    "CQ": {"key_bias": 2},
    "CB": {"bias_added": 1},
    "DST": STATS,
    "DNO": {"xn_ready": NB},
    "T": {"att_fill": 2, "xt_hi_ready": 2},
    "AKV": {"att_fill": 1, "k_silu": 1, "phik_ready": 1},
    "AQ": {"att_fill": 2, "phiq_hi": 2, "phiq_ready": 2},
    "AS": {"att_fill": 1},
    "AM": {"att_fill": 1, "m_hi_ready": 1},
    "AO": {"att_fill": 2},
    "CV": {"att_fill": 2, "v_hi_ready": 2},
    "CZ": {"att_fill": 2, "z_hi_ready": 2},
    "CS": {"att_fill": 1, "row_max": 2, "exp_bias": 1},
    "CP": {"att_fill": 1, "prob_hi_ready": 1},
    "CO": {"att_fill": 1, "inverse": 1},
    "CF": {"att_fill": 4, "tanh_done": 4, "out_ready": 1},
    "SCALE": {},
    "PREP": {"split_hi": 2, "split_lo": 2},
    "WIDE": {},
    "FOLD0": {"att_fill": 3},
    "TAKE0": {"fold_hi": 2},
    "FOLD1": {"att_fill": 3},
    "TAKE1": {"fold_hi": 1},
    "LOOK": {"look_max": 1, "look_sum": 1},
    "CHECK": {"att_fill": 1},
}
NOT_SEMAPHORES = {"ffn_fill", "att_fill", "a_tile"}


def added(step):
    kind, number, _ = step
    return ADDS[f"{kind}{number}" if kind in ("FOLD", "TAKE") else kind]


def steps_from(plan):
    steps = []
    for word in plan.split():
        who, _, name = word.rpartition(":")
        kind = name.rstrip("0123456789")
        digits = name[len(kind):]
        steps.append((kind, int(digits) if digits else 0, who))
    return steps


PLAN = steps_from("""
    U0 c:CST U1 U2 U3 c:CNO G0 c:T c:CB c:CQ G1 c:CV c:CZ G2 c:CS0 G3 c:CP0 c:CS1 c:CS2 c:CO0 c:CP1 c:CS3
    H0 c:CO1 c:CP2 H1 c:CO2 BST1 c:CP3 BNO1 a:AST H2 c:CO3 c:DST H3 BT1 c:DNO W0 c:T a:ANO U0 U1 c:CF a:T
    U2 U3 a:AB a:AKV0 a:AKV1 a:AKV2 G0 a:AKV3 G1 G2 a:AS a:AQ a:AM G3 a:AO H0 H1 n:BST0 n:BNO0 H2 H3 n:BT0
    W1""")


def only(*whose):
    return [s for s in PLAN if s[2] in whose]


def with_checks(steps, behind):
    out, behind = [], dict(behind)
    for s in steps:
        out.append(s)
        out += steps_from(behind.pop(s[:2], ""))
    return out


CHECKED = ["w12", "h1", "h2", "w3"]


def total(steps):
    out = {}
    for s in steps:
        for name, n in added(s).items():
            out[name] = out.get(name, 0) + n
    return out


LOOKS = [2 * KD * HID // LOOK, KH * HID // LOOK, KH * HID // LOOK, KH * D // LOOK]


class Counts:

    def __init__(self, start, rate=None, it=None):
        self.now, self.rate, self.it = dict(start), rate or {}, it
        self.seen = {}

    def value(self, name, k=0):
        v = self.now.get(name, 0) + k
        r = self.rate.get(name, 0)
        return v if self.it is None or not r else self.it * r + v

    def bank(self, ring, k):
        v = self.now.get(ring, 0) + k
        n, r = v // RING + 1, self.rate.get(ring, 0) // RING
        return v % RING, (n if self.it is None or not r else self.it * r + n)

    def ago(self, ring, kind, j):
        return self.seen[kind, j].get(ring, 0) - self.now.get(ring, 0)

    def ahead(self, step):
        self.seen[step[:2]] = dict(self.now)
        for name, n in added(step).items():
            self.now[name] = self.now.get(name, 0) + n


STAGE_OF = {"AST": "A", "BST": "B", "CST": "C", "DST": "C"}


def before(value):
    return None if isinstance(value, int) and value <= 1 else value - 1


PROLOGUE = steps_from("""
    a:AST a:ANO a:AB PREP a:T a:AKV0 SCALE a:AKV1 a:AKV2 a:AKV3 a:AS a:AQ a:AM a:AO FOLD0 WIDE
    n:BST0 n:BNO0 TAKE0 n:BT0 FOLD1 LOOK00 TAKE1 LOOK01 CHECK0 LOOK10 LOOK11""")
FIRST = with_checks(only("", "a", "n"), {
    ("U", 1): "LOOK12", ("U", 2): "LOOK13", ("U", 3): "CHECK1", ("G", 0): "LOOK20", ("G", 1): "LOOK21 LOOK22",
    ("G", 2): "LOOK23", ("G", 3): "CHECK2 LOOK30", ("H", 0): "CHECK3"})
BODY = PLAN
LAST = only("", "c")
TAIL = only("c")


def build(nc, a):
    with ExitStack() as ctx:
        def sb(name, shape, dt=F32):
            return ctx.enter_context(nc.sbuf_tensor(name, shape, dt))

        def sem(name):
            return ctx.enter_context(nc.semaphore(name))

        banks = {r: [ctx.enter_context(nc.psum_tensor(f"{r}_{b}", [P, 512], F32)) for b in range(RING)]
                 for r in ("ffn_fill", "att_fill")}

        w12 = sb("w12", [P, 2, KD, HID], F32R)
        h1 = sb("h1", [P, KH, HID], F32R)
        h2 = sb("h2", [P, KH, HID], F32R)
        w3 = sb("w3", [P, KH, D], F32R)
        checked = [w12[:].rearrange("p a k n -> p (a k n)"), h1[:].rearrange("p k n -> p (k n)"),
                   h2[:].rearrange("p k n -> p (k n)"), w3[:].rearrange("p k n -> p (k n)")]
        def hi_lo(name, shape):
            return [sb(f"{name}_{part}", shape, F32R) for part in ("hi", "lo")]

        wq = hi_lo("wq", [P, KD, D])
        wkv = hi_lo("wkv", [P, KD, 2 * D])
        wo = sb("wo", [P, KD, D])
        wz = hi_lo("wz", [P, KD, D])
        wvo = hi_lo("wvo", [P, KD, D])
        wf = hi_lo("wf", [P, KD, D])
        scales = sb("scales", [P, 4, KH])
        cols = sb("cols", [P, 4, KD])
        scaled_bq = sb("scaled_bq", [P, KD])
        z_bias = sb("z_bias", [P, KD + 1])
        rows = sb("rows", [P, 6, D])
        bv_row, bo_row, s3_row, bout_row, fb_row, u_row = (rows[:, r, :] for r in range(6))
        ident = sb("ident", [P, P])
        ones = sb("ones", [P, P])
        head_mask = sb("head_mask", [P, P])

        x = sb("x", [P, SLOTS, NB, D])
        xn_b = sb("xn_b", [P, HB, D])
        half_hi = sb("half_hi", [P, KD, HT], F32R)
        half_lo = sb("half_lo", [P, KD, HT], F32R)
        act_hi = [sb(f"act{n}_hi", [P, KH, HT], F32R) for n in range(2)]
        act_lo = [sb(f"act{n}_lo", [P, KH, HT], F32R) for n in range(2)]
        gated = sb("gated", [P, 2, 2, HT])
        whole = sb("whole", [P, WHOLES, 2, HT])
        w_tmp = xn_b
        xn = sb("xn", [P, NB, D])
        silu_q = xn[:].rearrange("p (k b) d -> p k (b d)", k=KD)
        xt = hi_lo("xt", [P, KD, S])
        qz = hi_lo("qz", [P, KD, S])
        kv_b = sb("kv_b", [P, NB, D])
        m_parts = sb("m_parts", [P, 2, KD, D], F32R)
        m_sb = [m_parts[:, 0], m_parts[:, 1]]
        values = [sb("values_hi", [P, NB, D], F32R), m_parts[:].rearrange("p h k d -> p (h k) d")]
        prob = kv_b[:].rearrange("p (r a) d -> p r (a d)", r=2)
        prob_t = hi_lo("prob_t", [P, NB, P])
        kv = sb("kv", [P, KD, P])
        st = sb("st", [P, NB, 6])
        mv_of = {w: sb(f"mv_{w}", [P, NB, 2]) for w in "ABC"}
        var_eps_of = {w: sb(f"var_eps_{w}", [P, NB]) for w in "ABC"}
        rstd_of = {w: sb(f"rstd_{w}", [P, NB]) for w in "ABC"}
        minus_half = sb("minus_half", [P, NB])
        cq = sb("cq", [P, 2, NB])
        sm = sb("sm", [P, 5, NB])
        lowsum = sb("lowsum", [P, 4, 2 * max(LOOKS)])
        flag = sb("flag", [P, 4])

        raw_wkv = kv_b[:].rearrange("p (k a) d -> p k (a d)", k=KD)
        raw_wq = gated[:, 0]
        raw = [x[:, 1 + n // 2, 2 * (n % 2):2 * (n % 2) + 2, :] for n in range(6)]
        raw_q, raw_k, raw_v, raw_out, raw_f, raw_a1 = raw
        spare = whole[:].rearrange("p a b n -> p (a b n)")
        raw_a2 = spare[:, 0:512].rearrange("p (k n) -> p k n", k=KD)
        t1 = gated[:, 1]
        bk_wide = spare[:, 512:768].rearrange("p (k n) -> p k n", k=KD)
        bv_wide = spare[:, 768:1024].rearrange("p (k n) -> p k n", k=KD)
        squares = kv_b[:].rearrange("p a d -> p (a d)")

        full = {r: [sem(f"{r}_full{b}") for b in range(RING)] for r in banks}
        taken = {r: [sem(f"{r}_taken{b}") for b in range(RING)] for r in banks}
        names = sorted({n for increments in ADDS.values() for n in increments} - NOT_SEMAPHORES)
        s = {n: sem(n) for n in names}
        x_loaded, x_stored = sem("x_loaded"), sem("x_stored")
        a_loaded, c_loaded, small_loaded = sem("a_loaded"), sem("c_loaded"), sem("small_loaded")
        w_bounced = [sem(f"{n}_bounced") for n in CHECKED]
        w_loaded = [sem(f"{n}_loaded") for n in CHECKED]
        consts, wide = sem("consts"), sem("wide")

        start = {}
        phases = []
        for steps in (PROLOGUE, FIRST):
            phases.append(dict(start))
            for n, k in total(steps).items():
                start[n] = start.get(n, 0) + k
        phases.append(dict(start))
        rate = total(BODY)
        for n, k in rate.items():
            start[n] = start.get(n, 0) + k * (T - 2)
        phases.append(dict(start))
        for n, k in total(LAST).items():
            start[n] = start.get(n, 0) + k
        phases.append(dict(start))

        def walk(eng, part):
            def steps_of(steps, counts, slots):
                for step in steps:
                    part(step, counts, slots)
                    counts.ahead(step)

            beginning = Counts(phases[0])
            steps_of(PROLOGUE, beginning, {"a": 0, "n": 0})
            steps_of(FIRST, beginning, {"": 0, "a": 1, "n": 1})
            with eng.Fori(0, T - 2) as it:
                steps_of(BODY, Counts(phases[2], rate, it),
                         {"c": eng.snap(it % SLOTS), "": eng.snap((it + 1) % SLOTS),
                          "a": eng.snap((it + 2) % SLOTS), "n": eng.snap((it + 2) % SLOTS)})
            steps_of(LAST, Counts(phases[3]), {"c": (T - 2) % SLOTS, "": (T - 1) % SLOTS})
            steps_of(TAIL, Counts(phases[4]), {"c": (T - 1) % SLOTS})

        def wait(eng, which, value):
            if value is not None and not (isinstance(value, int) and value <= 0):
                eng.wait_ge(which, value)

        def wait_apart(eng, which, value):
            if isinstance(value, int):
                eng.wait_ge(which, value)
            else:
                register = eng.to_reg(value)
                eng.wait_ge(consts, 7)
                eng.wait_ge(which, register)

        def to_fill(eng, c, ring, k):
            b, n = c.bank(ring, k)
            wait(eng, taken[ring][b], before(n))
            return banks[ring][b], full[ring][b]

        def filled(eng, c, ring, k):
            b, n = c.bank(ring, k)
            eng.wait_ge(full[ring][b], n)
            return banks[ring][b], taken[ring][b]

        def wait_taken(eng, c, ring, k):
            b, n = c.bank(ring, k)
            eng.wait_ge(taken[ring][b], n)

        two = lambda bank: bank[:].rearrange("p (a n) -> p a n", a=2)
        four = lambda bank: bank[:].rearrange("p (a n) -> p a n", a=4)
        def low_halves(j):
            halves = checked[j // 10].bitcast(U16).rearrange("p (n h) -> p n h", h=2)[:, :, 0]
            piece = halves[:, j % 10 * LOOK:(j % 10 + 1) * LOOK]
            return piece[:, :SQUARED], piece[:, SQUARED:]

        row2 = lambda row: row[:, None, :].broadcast_to([P, 2, D])

        block = ctx.enter_context(nc.Block())

        x_in = a["L0_attn_x"].rearrange("t (b p) d -> t p b d", p=P)
        x_out = a["out"].rearrange("t (b p) d -> t p b d", p=P)

        def km(name):
            return a[name].rearrange("(k p) n -> p k n", p=P)

        @block.sync
        def _(sp):
            sp.dma_start(x[:, 0], x_in[0]).then_inc(x_loaded, 16)
            sp.dma_start(raw_wkv[:, :, 0:D], km("wk0T")).then_inc(a_loaded, 16)
            sp.dma_start(raw_wkv[:, :, D:2 * D], km("wv0T")).then_inc(a_loaded, 16)
            sp.dma_start(raw_wq, km("wq0T")).then_inc(a_loaded, 16)
            sp.dma_start(wo[:], km("wo0T")).then_inc(a_loaded, 16)
            sp.dma_start(rows[:, 0:5, :], a["rows"][None].broadcast_to([P, 5, D])).then_inc(small_loaded, 16)
            sp.dma_start(cols[:], a["cols"]).then_inc(small_loaded, 16)
            sp.dma_start(scales[:], a["scales"]).then_inc(small_loaded, 16)
            parts = [[("w1T", w12[:, 0]), ("w2T", w12[:, 1])], [("h1T", h1[:])], [("h2T", h2[:])], [("w3T", w3[:])]]

            def bounce(layer):
                for name, _ in parts[layer]:
                    sp.dma_start(a["scratch_" + name], a[name]).then_inc(w_bounced[layer], 16)

            def land(layer):
                sp.wait_ge(w_bounced[layer], 16 * len(parts[layer]))
                for name, tile in parts[layer]:
                    sp.dma_start(tile.bitcast(F32), a["scratch_" + name].rearrange("(k p) n -> p k n", p=P))\
                      .then_inc(w_loaded[layer], 16)

            for tile, name in ((raw_q, "L1_attn_w_q"), (raw_k, "L1_attn_w_k"), (raw_v, "L1_attn_w_v"),
                               (raw_out, "woutT"), (raw_f, "wfT"), (raw_a1, "L1_ffn_aux_weight1"),
                               (raw_a2, "L1_ffn_aux_weight2")):
                sp.dma_start(tile, km(name)).then_inc(c_loaded, 16)
            bounce(0)
            bounce(1)
            land(0)
            land(1)
            bounce(2)
            land(2)
            bounce(3)
            land(3)
            c = Counts(phases[0])
            for step in PROLOGUE:
                if step[:2] == ("FOLD", 1):
                    wait_taken(sp, c, "att_fill", 2)
                c.ahead(step)
            for t in range(1, SLOTS):
                sp.dma_start(x[:, t], x_in[t]).then_inc(x_loaded, 16)
                sp.wait_ge(x_loaded, 16 * (t + 1))
            with sp.Fori(0, T - SLOTS) as t:
                slot = sp.snap(t % SLOTS)
                sp.wait_ge(s["out_ready"], t + 1)
                sp.dma_start(x_out[t], x[:, slot]).then_inc(x_stored, 16)
                wait_apart(sp, x_stored, 16 * t + 16)
                wait_apart(sp, x_loaded, 16 * t + 16 * SLOTS)
                sp.dma_start(x[:, slot], x_in[t + SLOTS]).then_inc(x_loaded, 16)
            for t in range(T - SLOTS, T):
                sp.wait_ge(s["out_ready"], t + 1)
                sp.dma_start(x_out[t], x[:, t % SLOTS]).then_inc(x_stored, 16)
            sp.wait_ge(x_stored, 16 * T)

        @block.gpsimd
        def _(pool):
            pool.memset(ident[:], 0.0).then_inc(consts, 1)
            pool.memset(head_mask[:], 1.0).then_inc(consts, 1)
            pool.memset(ones[:], 1.0).then_inc(consts, 1)
            pool.memset(minus_half[:], -0.5).then_inc(consts, 1)
            pool.wait_ge(consts, 4)
            pool.affine_select(out=ident[:], in_=ident[:], compare_op=ALU.not_equal, fill=1.0, base=0,
                               pattern=[[-1, P]], channel_multiplier=1).then_inc(consts, 1)
            hm = head_mask[:].rearrange("p (g r) -> p g r", r=HEAD)
            pool.affine_select(out=hm, in_=hm, compare_op=ALU.is_ge, fill=0.0, base=0,
                               pattern=[[-HEAD, P // HEAD], [0, HEAD]], channel_multiplier=1).then_inc(consts, 1)
            pool.wait_ge(consts, 6)
            pool.affine_select(out=hm, in_=hm, compare_op=ALU.is_ge, fill=0.0, base=HEAD - 1,
                               pattern=[[HEAD, P // HEAD], [0, HEAD]], channel_multiplier=-1).then_inc(consts, 1)

            def add_bias(c, xs, bias_row):
                pool.wait_ge(small_loaded, 16 * 3)
                wait_apart(pool, s["xn_ready"], c.value("xn_ready"))
                for b in range(0, NB, 2):
                    last = pool.tensor_tensor(xs[:, b:b + 2, :], xs[:, b:b + 2, :], row2(bias_row), ALU.add)
                last.then_inc(s["bias_added"], 1)

            def inverse_deviation(c, stage, nb):
                wait_apart(pool, s["ln_stats"], c.value("ln_stats", 3))
                pool.tensor_tensor(rstd_of[stage][:, :nb], var_eps_of[stage][:, :nb], minus_half[:, :nb], ALU.pow)\
                    .then_inc(s["ln_pow"], 1)

            def part(step, c, slots):
                kind, j, who = step
                if kind in STAGE_OF:
                    inverse_deviation(c, STAGE_OF[kind], HB if kind == "BST" else NB)
                elif kind in ("AB", "CB"):
                    add_bias(c, x[:, slots[who]], bo_row if kind == "AB" else bout_row)
                elif kind == "U":
                    n = c.now.get("ffn_ready", 0)
                    pool.wait_ge(s["hi_ready"], c.value("hi_ready", 1))
                    blocks = slice(2 * j, 2 * j + 2)
                    pool.tensor_tensor(act_lo[0][:, blocks], whole[:, n % WHOLES], act_hi[0][:, blocks].bitcast(F32),
                                       ALU.subtract).then_inc(s["ffn_ready"], 1)
                elif kind == "CF":
                    for b in range(NB):
                        wait_apart(pool, s["tanh_done"], c.value("tanh_done", b + 1))
                        xb = x[:, slots[who], b, :]
                        last = pool.tensor_tensor(xb, xb, kv_b[:, b, :], ALU.add)
                    last.then_inc(s["out_ready"], 1)

            walk(pool, part)

        @block.vector
        def _(dve):
            def statistics(c, xs, stage, nb):
                mv = mv_of[stage]
                for b in range(nb):
                    last = dve.bn_stats(st[:, b, :], xs[:, b, :])
                last.then_inc(s["ln_stats"], 1)
                wait_apart(dve, s["ln_stats"], c.value("ln_stats", 1))
                for b in range(nb):
                    last = dve.bn_aggr(mv[:, b, :], st[:, b, :])
                last.then_inc(s["ln_stats"], 1)
                dve.wait_ge(s["ln_stats"], c.value("ln_stats", 2))
                dve.tensor_scalar(var_eps_of[stage][:, :nb], mv[:, :nb, 1], EPS, None, ALU.add)\
                   .then_inc(s["ln_stats"], 1)

            def normalise(c, xs, out, stage, nb):
                dve.wait_ge(s["ln_pow"], c.value("ln_pow"))
                for b in range(nb):
                    dve.tensor_scalar(out[:, b, :], xs[:, b, :], mv_of[stage][:, b, 0:1],
                                      rstd_of[stage][:, b:b + 1], ALU.subtract, ALU.mult).then_inc(s["xn_ready"], 1)

            def part(step, c, slots):
                kind, j, who = step
                if kind == "AST":
                    wait_apart(dve, x_loaded, c.value("a_tile", 1) * 16)
                    statistics(c, x[:, slots[who]], "A", NB)
                elif kind == "CST":
                    wait_apart(dve, s["b_done"], c.value("b_done"))
                    statistics(c, x[:, slots[who]], "C", NB)
                elif kind in ("ANO", "CNO", "DNO"):
                    normalise(c, x[:, slots[who]], xn, "A" if kind == "ANO" else "C", NB)
                elif kind == "CQ":
                    dve.wait_ge(s["xn_ready"], c.value("xn_ready"))
                    for b in range(NB):
                        last = dve.tensor_tensor_reduce(kv_b[:, b, :], xn[:, b, :], u_row, 1.0, 0.0,
                                                        ALU.mult, ALU.add, cq[:, 0, b:b + 1])
                    last.then_inc(s["key_bias"], 1)
                    dve.wait_ge(s["key_bias"], c.value("key_bias", 1))
                    dve.tensor_scalar(cq[:, 1, :], cq[:, 0, :], z_bias[:, KD:KD + 1], None, ALU.add)\
                       .then_inc(s["key_bias"], 1)
                elif kind == "DST":
                    b, n = c.bank("att_fill", c.ago("att_fill", "CO", NB - 1))
                    wait_apart(dve, taken["att_fill"][b], n)
                    statistics(c, x[:, slots[who]], "C", NB)
                elif kind == "BST":
                    xs = x[:, slots[who]]
                    if j == 0:
                        b, n = c.bank("att_fill", c.ago("att_fill", "AO", 0) + 1)
                        wait_apart(dve, taken["att_fill"][b], n)
                    statistics(c, xs[:, HB * j:HB * j + HB], "B", HB)
                elif kind == "BNO":
                    normalise(c, x[:, slots[who], HB * j:HB * j + HB], xn_b, "B", HB)
                elif kind == "T":
                    for k in range(KD):
                        bank, out = filled(dve, c, "att_fill", k)
                        dve.wait_ge(s["xt_hi_ready"], c.value("xt_hi_ready", k + 1))
                        dve.tensor_tensor(xt[1][:, k, :], bank[:], xt[0][:, k, :].bitcast(F32), ALU.subtract)\
                           .then_inc(out, 1)
                elif kind == "BT":
                    bank, out = filled(dve, c, "ffn_fill", 0)
                    dve.wait_ge(s["bt_hi"], c.value("bt_hi", 1))
                    dve.tensor_tensor(half_lo[:], two(bank), half_hi[:].bitcast(F32), ALU.subtract).then_inc(out, 1)
                elif kind == "U":
                    n = c.now.get("ffn_ready", 0)
                    wait_taken(dve, c, "ffn_fill", 0)
                    bank, out = filled(dve, c, "ffn_fill", 1)
                    wait(dve, s["ffn_ready"], c.value("ffn_ready", 1 - WHOLES))
                    for o in range(2):
                        last = dve.scalar_tensor_tensor(whole[:, n % WHOLES, o, :], two(bank)[:, o, :],
                                                        scales[:, 1, 2 * j + o:2 * j + o + 1],
                                                        gated[:, j % 2, o, :], ALU.mult, ALU.mult)
                    last.then_inc(out, 1)
                    wait_taken(dve, c, "ffn_fill", 1)
                    dve.tensor_copy(act_hi[0][:, 2 * j:2 * j + 2], whole[:, n % WHOLES]).then_inc(s["hi_ready"], 1)
                elif kind in ("G", "H"):
                    n, dst, blocks = c.now.get("ffn_ready", 0), 1 if kind == "G" else 0, slice(2 * j, 2 * j + 2)
                    wait_taken(dve, c, "ffn_fill", 0)
                    dve.tensor_copy(act_hi[dst][:, blocks], whole[:, n % WHOLES]).then_inc(s["hi_ready"], 1)
                    dve.wait_ge(s["hi_ready"], c.value("hi_ready", 1))
                    dve.tensor_tensor(act_lo[dst][:, blocks], whole[:, n % WHOLES], act_hi[dst][:, blocks].bitcast(F32),
                                      ALU.subtract).then_inc(s["ffn_ready"], 1)
                elif kind == "W":
                    bank, out = filled(dve, c, "ffn_fill", 0)
                    dve.tensor_tensor(w_tmp[:], two(bank), row2(s3_row), ALU.mult).then_inc(out, 1)
                    wait_taken(dve, c, "ffn_fill", 0)
                    xs = x[:, slots[who], HB * j:HB * j + HB, :]
                    dve.tensor_tensor(xs, xs, w_tmp[:], ALU.add).then_inc(s["b_done"], 1)
                elif kind == "AKV":
                    if j == 0 and c.it is None:
                        dve.wait_ge(small_loaded, 16 * 3)
                    if j == 0:
                        wait(dve, s["out_ready"], c.value("out_ready"))
                    dve.wait_ge(s["k_silu"], c.value("k_silu", 1))
                    bank, out = filled(dve, c, "att_fill", 0)
                    dve.tensor_tensor(kv_b[:, j, :], bank[:, D:2 * D], bv_row, ALU.add).then_inc(out, 1)
                    dve.tensor_scalar(xn[:, j, :], xn[:, j, :], 1.0, None, ALU.add).then_inc(s["phik_ready"], 1)
                elif kind == "AQ":
                    for k in range(KD):
                        wait_taken(dve, c, "att_fill", k)
                        dve.tensor_scalar(qz[0][:, k, :], silu_q[:, k, :], 1.0, None, ALU.add)\
                           .then_inc(s["phiq_hi"], 1)
                        dve.wait_ge(s["phiq_hi"], c.value("phiq_hi", k + 1))
                        dve.scalar_tensor_tensor(qz[1][:, k, :], silu_q[:, k, :], 1.0, qz[0][:, k, :].bitcast(F32),
                                                 ALU.add, ALU.subtract).then_inc(s["phiq_ready"], 1)
                elif kind == "SCALE":
                    dve.tensor_scalar(scaled_bq[:], cols[:, 0, :], HEAD ** -0.25, None, ALU.mult).then_inc(wide, 1)
                elif kind == "AS":
                    if c.it is None:
                        dve.wait_ge(consts, 7)
                    bank, out = filled(dve, c, "att_fill", 0)
                    dve.tensor_tensor(kv[:], four(bank)[:, 0:2, :], head_mask[:, None, :].broadcast_to([P, 2, P]),
                                      ALU.mult).then_inc(out, 1)
                elif kind == "AM":
                    bank, out = filled(dve, c, "att_fill", 0)
                    dve.wait_ge(s["m_hi_ready"], c.value("m_hi_ready", 1))
                    dve.tensor_tensor(m_sb[1], two(bank), m_sb[0].bitcast(F32), ALU.subtract).then_inc(out, 1)
                elif kind == "CZ":
                    for k in range(KD):
                        bank, out = filled(dve, c, "att_fill", k)
                        dve.wait_ge(s["z_hi_ready"], c.value("z_hi_ready", k + 1))
                        dve.scalar_tensor_tensor(qz[1][:, k, :], bank[:], z_bias[:, k:k + 1],
                                                 qz[0][:, k, :].bitcast(F32), ALU.add, ALU.subtract).then_inc(out, 1)
                elif kind == "AO":
                    dve.wait_ge(s["bias_added"], c.value("bias_added"))
                    for g in range(2):
                        bank, out = filled(dve, c, "att_fill", g)
                        xs = x[:, slots[who], 2 * g:2 * g + 2, :]
                        dve.tensor_tensor(xs, two(bank), xs, ALU.add).then_inc(out, 1)
                elif kind == "CV":
                    for g in range(2):
                        bank, out = filled(dve, c, "att_fill", g)
                        dve.wait_ge(s["v_hi_ready"], c.value("v_hi_ready", g + 1))
                        blocks = slice(2 * g, 2 * g + 2)
                        dve.tensor_tensor(values[1][:, blocks, :], two(bank), values[0][:, blocks, :].bitcast(F32),
                                          ALU.subtract).then_inc(out, 1)
                elif kind == "CP":
                    bank, out = filled(dve, c, "att_fill", 0)
                    dve.wait_ge(s["prob_hi_ready"], c.value("prob_hi_ready", 1))
                    dve.tensor_tensor(prob_t[1][:], four(bank), prob_t[0][:].bitcast(F32), ALU.subtract)\
                       .then_inc(out, 1)
                elif kind == "CS":
                    bank, _ = filled(dve, c, "att_fill", 0)
                    q = slice(j, j + 1)
                    dve.tensor_reduce(sm[:, 0, q], bank[:], AX.X, ALU.max).then_inc(s["row_max"], 1)
                    dve.wait_ge(s["row_max"], c.value("row_max", 1))
                    dve.scalar_tensor_tensor(sm[:, 1, q], sm[:, 0, q], cq[:, 1, q], cq[:, 1, q],
                                             ALU.add, ALU.subtract).then_inc(s["row_max"], 1)
                    dve.wait_ge(s["row_max"], c.value("row_max", 2))
                    dve.tensor_scalar(sm[:, 2, q], sm[:, 1, q], -float(D) ** -0.5, None, ALU.mult)\
                       .then_inc(s["exp_bias"], 1)
                elif kind == "CO":
                    q = slice(j, j + 1)
                    bank, out = filled(dve, c, "att_fill", 0)
                    dve.reciprocal(sm[:, 4, q], sm[:, 3, q]).then_inc(s["inverse"], 1)
                    dve.wait_ge(s["inverse"], c.value("inverse", 1))
                    dve.wait_ge(s["bias_added"], c.value("bias_added"))
                    xs = x[:, slots[who], j, :]
                    dve.scalar_tensor_tensor(xs, bank[:, 0:D], sm[:, 4, q], xs, ALU.mult, ALU.add).then_inc(out, 1)
                elif kind == "CF":
                    for b in range(NB):
                        bank, out = filled(dve, c, "att_fill", b)
                        dve.tensor_tensor(kv_b[:, b, :], bank[:, 0:D], fb_row, ALU.add).then_inc(out, 1)
                elif kind == "PREP":
                    for n, (whole_w, parts_w) in enumerate(((raw_wkv, wkv), (raw_wq, wq))):
                        dve.wait_ge(s["split_hi"], n + 1)
                        dve.tensor_tensor(parts_w[1][:], whole_w, parts_w[0][:].bitcast(F32), ALU.subtract)\
                           .then_inc(s["split_lo"], 1)
                elif kind == "WIDE":
                    for k in range(KD):
                        dve.tensor_scalar(bk_wide[:, k, :], ones[:], cols[:, 2, k:k + 1], None, ALU.mult)\
                           .then_inc(wide, 1)
                        dve.tensor_scalar(bv_wide[:, k, :], ones[:], cols[:, 3, k:k + 1], None, ALU.mult)\
                           .then_inc(wide, 1)
                elif kind == "TAKE":
                    first = c.ago("att_fill", "FOLD", j)

                    def take_split(k, dst, nth):
                        bank, out = filled(dve, c, "att_fill", first + k)
                        dve.tensor_copy(dst[0][:], two(bank)).then_inc(s["fold_hi"], 1)
                        dve.wait_ge(s["fold_hi"], nth)
                        dve.tensor_tensor(dst[1][:], two(bank), dst[0][:].bitcast(F32), ALU.subtract).then_inc(out, 1)

                    if j == 0:
                        bank, out = filled(dve, c, "att_fill", first)
                        dve.tensor_copy(t1, two(bank)).then_inc(out, 1)
                        take_split(1, wz, 1)
                        take_split(2, wvo, 2)
                    else:
                        bank, out = filled(dve, c, "att_fill", first)
                        dve.tensor_copy(z_bias[:], bank[:, 0:KD + 1]).then_inc(out, 1)
                        bank, out = filled(dve, c, "att_fill", first + 1)
                        dve.tensor_copy(u_row, two(bank)[:, 1, :])
                        dve.tensor_tensor(bout_row, two(bank)[:, 0, :], bout_row, ALU.add).then_inc(out, 1)
                        take_split(2, wf, 3)
                elif kind == "LOOK":
                    dve.wait_ge(w_loaded[j // 10], 16 * (2 if j < 10 else 1))
                    dve.tensor_reduce(lowsum[:, j // 10, 2 * (j % 10):2 * (j % 10) + 1], low_halves(j)[1],
                                      AX.X, ALU.max).then_inc(s["look_max"], 1)
                elif kind == "CHECK":
                    bank, out = filled(dve, c, "att_fill", 0)
                    dve.tensor_reduce(flag[:, j:j + 1], bank[:, 0:2 * LOOKS[j]], AX.X, ALU.add).then_inc(out, 1)

            walk(dve, part)

        @block.scalar
        def _(act):
            def part(step, c, slots):
                kind, j, who = step
                if kind == "T":
                    for k in range(KD):
                        bank, _ = filled(act, c, "att_fill", k)
                        act.activation(xt[0][:, k, :], bank[:], ACT.Copy).then_inc(s["xt_hi_ready"], 1)
                elif kind == "BT":
                    bank, _ = filled(act, c, "ffn_fill", 0)
                    act.activation(half_hi[:], two(bank), ACT.Copy).then_inc(s["bt_hi"], 1)
                elif kind == "U":
                    if j >= 2:
                        wait_taken(act, c, "ffn_fill", -3)
                    bank, out = filled(act, c, "ffn_fill", 0)
                    for o in range(2):
                        last = act.activation(gated[:, j % 2, o, :], two(bank)[:, o, :], ACT.Silu,
                                              scale=scales[:, 0, 2 * j + o:2 * j + o + 1])
                    last.then_inc(out, 1)
                elif kind in ("G", "H"):
                    n = c.now.get("ffn_ready", 0)
                    act.wait_ge(s["ffn_ready"], c.value("ffn_ready", 1 - WHOLES))
                    bank, out = filled(act, c, "ffn_fill", 0)
                    layer = 2 if kind == "G" else 3
                    for o in range(2):
                        last = act.activation(whole[:, n % WHOLES, o, :], two(bank)[:, o, :], ACT.Gelu,
                                              scale=scales[:, layer, 2 * j + o:2 * j + o + 1])
                    last.then_inc(out, 1)
                elif kind == "AKV":
                    bank, _ = filled(act, c, "att_fill", 0)
                    act.activation(xn[:, j, :], bank[:, 0:D], ACT.Silu, scale=HEAD ** -0.25)\
                       .then_inc(s["k_silu"], 1)
                elif kind == "AQ":
                    act.wait_ge(wide, 1)
                    for k in range(KD):
                        bank, out = filled(act, c, "att_fill", k)
                        act.activation(silu_q[:, k, :], bank[:], ACT.Silu, bias=scaled_bq[:, k:k + 1],
                                       scale=HEAD ** -0.25).then_inc(out, 1)
                elif kind == "CV":
                    for g in range(2):
                        bank, _ = filled(act, c, "att_fill", g)
                        act.activation(values[0][:, 2 * g:2 * g + 2, :], two(bank), ACT.Copy)\
                           .then_inc(s["v_hi_ready"], 1)
                elif kind == "AM":
                    bank, _ = filled(act, c, "att_fill", 0)
                    act.activation(m_sb[0], two(bank), ACT.Copy).then_inc(s["m_hi_ready"], 1)
                elif kind == "CZ":
                    for k in range(KD):
                        bank, _ = filled(act, c, "att_fill", k)
                        act.activation(qz[0][:, k, :], bank[:], ACT.Identity, bias=z_bias[:, k:k + 1])\
                           .then_inc(s["z_hi_ready"], 1)
                elif kind == "CS":
                    bank, out = filled(act, c, "att_fill", 0)
                    act.wait_ge(s["exp_bias"], c.value("exp_bias", 1))
                    q = slice(j, j + 1)
                    act.activation(prob[:, j % 2, :], bank[:], ACT.Exp, bias=sm[:, 2, q], scale=float(D) ** -0.5,
                                   accum_out=sm[:, 3, q]).then_inc(out, 1)
                elif kind == "CP":
                    bank, _ = filled(act, c, "att_fill", 0)
                    act.activation(prob_t[0][:], four(bank), ACT.Copy).then_inc(s["prob_hi_ready"], 1)
                elif kind == "CF":
                    for b in range(NB):
                        wait_taken(act, c, "att_fill", b)
                        act.activation(kv_b[:, b, :], kv_b[:, b, :], ACT.Tanh).then_inc(s["tanh_done"], 1)
                elif kind == "LOOK":
                    act.wait_ge(w_loaded[j // 10], 16 * (2 if j < 10 else 1))
                    wait(act, s["look_sum"], c.value("look_sum"))
                    act.activation(squares[:, :SQUARED], low_halves(j)[0], ACT.Square,
                                   accum_out=lowsum[:, j // 10, 2 * (j % 10) + 1:2 * (j % 10) + 2])\
                       .then_inc(s["look_sum"], 1)
                elif kind == "PREP":
                    act.wait_ge(a_loaded, 16 * 4)
                    act.activation(wkv[0][:], raw_wkv, ACT.Copy).then_inc(s["split_hi"], 1)
                    act.activation(wq[0][:], raw_wq, ACT.Copy).then_inc(s["split_hi"], 1)

            walk(act, part)

        @block.tensor
        def _(pe):
            flags = {}

            def product(out, pairs):
                for n, (lhsT, rhs) in enumerate(pairs):
                    last = pe.matmul(out, lhsT, rhs, start=n == 0, stop=n == len(pairs) - 1)
                return last

            def pairs3(lhsT, rhs):
                return [(lhsT[0], rhs[0]), (lhsT[0], rhs[1]), (lhsT[1], rhs[0])]

            def product3(out, blocks):
                return product(out, [pair for lhsT, rhs in blocks for pair in pairs3(lhsT, rhs)])

            def of(parts, *index):
                return [part[(slice(None), *index)] for part in parts]

            def ffn_products(c, layer, emit):
                if layer not in flags:
                    wait_taken(pe, c, "att_fill", c.ago("att_fill", "CHECK", layer))
                    flags[layer] = pe.value_load(flag[0:1, layer:layer + 1].bitcast(I32))
                with pe.If(flags[layer] != 0):
                    emit(lambda ap: ap.bitcast(F32))
                with pe.Else():
                    emit(lambda ap: ap)

            def hidden(c, layer, weights, src, j):
                bank, done = to_fill(pe, c, "ffn_fill", 0)

                def emit(view):
                    for k in range(KH):
                        if j == 0 and k % 2 == 0:
                            pe.wait_ge(s["ffn_ready"], c.value("ffn_ready", k // 2 + 1 - PAIRS))
                        for o in range(2):
                            w = weights[:, k, (2 * j + o) * P:(2 * j + o + 1) * P]
                            for half, moving in enumerate((act_hi[src], act_lo[src])):
                                last = pe.matmul(two(bank)[:, o, :], view(w), view(moving[:, k, :]),
                                                 start=k == 0 and o == 0 and half == 0,
                                                 stop=k == KH - 1 and half == 1, skip_group_check=True)
                    last.then_inc(done, 1)

                ffn_products(c, layer, emit)

            def part(step, c, slots):
                kind, j, who = step
                if kind == "T":
                    norm = "ANO" if who == "a" else "DNO" if ("DNO", 0) in c.seen else "CNO"
                    pair = [to_fill(pe, c, "att_fill", k) for k in range(KD)]
                    for b in range(NB):
                        pe.wait_ge(s["xn_ready"], c.value("xn_ready", c.ago("xn_ready", norm, 0) + b + 1))
                        for k, (bank, done) in enumerate(pair):
                            last = pe.transpose(four(bank)[:, b, :], xn[:, b, k * P:(k + 1) * P], ident[:])
                            if b == NB - 1:
                                last.then_inc(done, 1)
                elif kind == "BT":
                    bank, done = to_fill(pe, c, "ffn_fill", 0)
                    for b in range(HB):
                        pe.wait_ge(s["xn_ready"], c.value("xn_ready", c.ago("xn_ready", "BNO", j) + b + 1))
                        for k in range(KD):
                            last = pe.transpose(two(bank)[:, k, b * P:(b + 1) * P],
                                                xn_b[:, b, k * P:(k + 1) * P], ident[:])
                    last.then_inc(done, 1)
                elif kind == "U":
                    if j == 0:
                        wait_taken(pe, c, "ffn_fill", -1 if c.it is None and c.now["ffn_fill"] == 1 else -2)
                    a_bank, a_done = to_fill(pe, c, "ffn_fill", 0)
                    b_bank, b_done = to_fill(pe, c, "ffn_fill", 1)

                    def emit(view):
                        for which, (bank, done) in enumerate(((a_bank, a_done), (b_bank, b_done))):
                            for o in range(2):
                                cols_o = slice((2 * j + o) * P, (2 * j + o + 1) * P)
                                last = product(two(bank)[:, o, :],
                                               [(view(w12[:, which, k, cols_o]), view(moving[:, k, :]))
                                                for k in range(KD) for moving in (half_hi, half_lo)])
                            last.then_inc(done, 1)

                    ffn_products(c, 0, emit)
                elif kind == "G":
                    hidden(c, 1, h1, 0, j)
                elif kind == "H":
                    hidden(c, 2, h2, 1, j)
                elif kind == "W":
                    bank, done = to_fill(pe, c, "ffn_fill", 0)

                    def emit(view):
                        for k in range(KH):
                            if k % 2 == 0:
                                pe.wait_ge(s["ffn_ready"], c.value("ffn_ready", k // 2 + 1 - PAIRS))
                            for b in range(HB):
                                for half, part_of in enumerate((act_hi[0], act_lo[0])):
                                    last = pe.matmul(two(bank)[:, b, :], view(part_of[:, k, b * P:(b + 1) * P]),
                                                     view(w3[:, k, :]), start=k == 0 and b == 0 and half == 0,
                                                     stop=k == KH - 1 and half == 1, skip_group_check=True)
                        last.then_inc(done, 1)

                    ffn_products(c, 3, emit)
                elif kind == "AKV":
                    if j == 0:
                        for k in range(KD):
                            wait_taken(pe, c, "att_fill", k - 2)
                        if c.it is None:
                            pe.wait_ge(s["split_lo"], 1)
                    bank, done = to_fill(pe, c, "att_fill", 0)
                    tok = slice(j * P, (j + 1) * P)
                    product3(bank[:], [(of(xt, k, tok), of(wkv, k, slice(None))) for k in range(KD)])\
                        .then_inc(done, 1)
                elif kind == "AQ":
                    if c.it is None:
                        pe.wait_ge(s["split_lo"], 2)
                    for o in range(KD):
                        bank, done = to_fill(pe, c, "att_fill", o)
                        out_o = slice(o * P, (o + 1) * P)
                        product3(bank[:], [(of(wq, k, out_o), of(xt, k, slice(None))) for k in range(KD)])\
                            .then_inc(done, 1)
                elif kind == "AS":
                    pe.wait_ge(s["phik_ready"], c.value("phik_ready"))
                    bank, done = to_fill(pe, c, "att_fill", 0)
                    for g in range(KD):
                        cols_g = slice(g * P, (g + 1) * P)
                        last = product(four(bank)[:, g, :],
                                       [(kv_b[:, b, cols_g], xn[:, b, cols_g]) for b in range(NB)])
                    last.then_inc(done, 1)
                elif kind == "AM":
                    wait_taken(pe, c, "att_fill", c.ago("att_fill", "AS", 0))
                    bank, done = to_fill(pe, c, "att_fill", 0)
                    for g in range(KD):
                        last = product(two(bank)[:, g, :], [(kv[:, g, :], wo[:, g, :])])
                    last.then_inc(done, 1)
                elif kind == "AO":
                    wait_taken(pe, c, "att_fill", c.ago("att_fill", "AM", 0))
                    pe.wait_ge(s["phiq_ready"], c.value("phiq_ready"))
                    for g in range(2):
                        bank, done = to_fill(pe, c, "att_fill", g)
                        for b in range(2):
                            tok = slice((2 * g + b) * P, (2 * g + b + 1) * P)
                            last = product3(two(bank)[:, b, :],
                                            [(of(qz, k, tok), of(m_sb, k, slice(None))) for k in range(KD)])
                        last.then_inc(done, 1)
                elif kind == "CV":
                    for k in range(KD):
                        wait_taken(pe, c, "att_fill", c.ago("att_fill", "T", 0) + k)
                    for g in range(2):
                        bank, done = to_fill(pe, c, "att_fill", g)
                        for b in range(2):
                            tok = slice((2 * g + b) * P, (2 * g + b + 1) * P)
                            last = product3(two(bank)[:, b, :],
                                            [(of(xt, k, tok), of(wvo, k, slice(None))) for k in range(KD)])
                        last.then_inc(done, 1)
                elif kind == "CZ":
                    for o in range(KD):
                        bank, done = to_fill(pe, c, "att_fill", o)
                        out_o = slice(o * P, (o + 1) * P)
                        product3(bank[:], [(of(wz, k, out_o), of(xt, k, slice(None))) for k in range(KD)])\
                            .then_inc(done, 1)
                elif kind == "CS":
                    if j == 0:
                        for k in range(KD):
                            wait_taken(pe, c, "att_fill", c.ago("att_fill", "CZ", 0) + k)
                    bank, done = to_fill(pe, c, "att_fill", 0)
                    tok = slice(j * P, (j + 1) * P)
                    product3(bank[:], [(of(qz, k, tok), of(xt, k, slice(None))) for k in range(KD)])\
                        .then_inc(done, 1)
                elif kind == "CP":
                    wait_taken(pe, c, "att_fill", c.ago("att_fill", "CS", j))
                    bank, done = to_fill(pe, c, "att_fill", 0)
                    for b in range(NB):
                        last = pe.transpose(four(bank)[:, b, :], prob[:, j % 2, b * P:(b + 1) * P], ident[:])
                    last.then_inc(done, 1)
                elif kind == "CO":
                    if j == 0:
                        for g in range(2):
                            wait_taken(pe, c, "att_fill", c.ago("att_fill", "CV", 0) + g)
                    wait_taken(pe, c, "att_fill", c.ago("att_fill", "CP", j))
                    bank, done = to_fill(pe, c, "att_fill", 0)
                    everything = slice(None)
                    product3(bank[:, 0:D], [(of(prob_t, b, everything), of(values, b, everything)) for b in range(NB)])\
                        .then_inc(done, 1)
                elif kind == "CF":
                    for k in range(KD):
                        wait_taken(pe, c, "att_fill", c.ago("att_fill", "T", 0) + k)
                    for b in range(NB):
                        bank, done = to_fill(pe, c, "att_fill", b)
                        tok = slice(b * P, (b + 1) * P)
                        product3(bank[:, 0:D], [(of(xt, k, tok), of(wf, k, slice(None))) for k in range(KD)])\
                            .then_inc(done, 1)
                elif kind == "FOLD" and j == 0:
                    pe.wait_ge(c_loaded, 16 * 7)
                    blk = lambda o: slice(o * P, (o + 1) * P)
                    for n, (left, right) in enumerate(((raw_a1, raw_f), (raw_q, raw_k), (raw_v, raw_out))):
                        bank, done = to_fill(pe, c, "att_fill", n)
                        for o in range(KD):
                            last = product(two(bank)[:, o, :], [(left[:, k, blk(o)], right[:, k, :]) for k in range(KD)])
                        last.then_inc(done, 1)
                elif kind == "FOLD":
                    blk = lambda o: slice(o * P, (o + 1) * P)
                    pe.wait_ge(wide, 5)
                    bank, done = to_fill(pe, c, "att_fill", 0)
                    for o in range(KD):
                        product(bank[:, o:o + 1], [(raw_k[:, k, blk(o)], cols[:, 1, k:k + 1]) for k in range(KD)])
                    product(bank[:, KD:KD + 1], [(bk_wide[:, k, :], cols[:, 1, k:k + 1]) for k in range(KD)])\
                        .then_inc(done, 1)
                    bank, done = to_fill(pe, c, "att_fill", 1)
                    product(two(bank)[:, 0, :], [(bv_wide[:, k, :], raw_out[:, k, :]) for k in range(KD)])
                    product(two(bank)[:, 1, :], [(bk_wide[:, k, :], raw_q[:, k, :]) for k in range(KD)])\
                        .then_inc(done, 1)
                    wait_taken(pe, c, "att_fill", c.ago("att_fill", "FOLD", 0))
                    bank, done = to_fill(pe, c, "att_fill", 2)
                    for o in range(KD):
                        last = product(two(bank)[:, o, :], [(t1[:, k, blk(o)], raw_a2[:, k, :]) for k in range(KD)])
                    last.then_inc(done, 1)
                elif kind == "CHECK":
                    pe.wait_ge(s["look_max"], c.value("look_max"))
                    pe.wait_ge(s["look_sum"], c.value("look_sum"))
                    bank, done = to_fill(pe, c, "att_fill", 0)
                    product(bank[:, 0:2 * LOOKS[j]], [(ones[:], lowsum[:, j, 0:2 * LOOKS[j]])]).then_inc(done, 1)

            pe.wait_ge(consts, 7)
            walk(pe, part)


def kernel(**inputs):
    import concourse.bacc as bacc
    from concourse.bass_utils import run_bass_kernel_spmd

    def t(name):
        return np.ascontiguousarray(np.asarray(inputs[name]).T)

    def columns(*names):
        return np.ascontiguousarray(np.stack([np.asarray(inputs[name]).reshape(-1, P).T for name in names], axis=1))

    given = {
        "wq0T": t("L0_attn_Wq"), "wk0T": t("L0_attn_Wk"), "wv0T": t("L0_attn_Wv"), "wo0T": t("L0_attn_Wo"),
        "cols": columns("L0_attn_bq", "L1_attn_b_q", "L1_attn_b_k", "L1_attn_b_v"),
        "scales": columns("L0_ffn_w1_s", "L0_ffn_w2_s", "L0_ffn_h1_s", "L0_ffn_h2_s"),
        "rows": np.stack([np.asarray(inputs[name]) for name in (
            "L0_attn_bv", "L0_attn_bo", "L0_ffn_w3_s", "L1_attn_b_out", "L1_ffn_bias")]),
        "w1T": t("L0_ffn_w1_w"), "w2T": t("L0_ffn_w2_w"), "h1T": t("L0_ffn_h1_w"), "h2T": t("L0_ffn_h2_w"),
        "w3T": t("L0_ffn_w3_w"), "woutT": t("L1_attn_w_out"), "wfT": t("L1_ffn_weight"),
    }
    for name in ("L0_attn_x", "L1_attn_w_q", "L1_attn_w_k", "L1_attn_w_v", "L1_ffn_aux_weight1",
                 "L1_ffn_aux_weight2"):
        given[name] = np.ascontiguousarray(inputs[name])
    nc = bacc.Bacc("TRN2", target_bir_lowering=False, num_devices=1, dynamic_dma_scratch_size=1024)
    arrays, args = {}, {}
    for name, array in given.items():
        arrays["in_" + name] = array
        args[name] = nc.dram_tensor("in_" + name, array.shape, F32, kind="ExternalInput").ap()
    for name in ("w1T", "w2T", "h1T", "h2T", "w3T"):
        args["scratch_" + name] = nc.dram_tensor("scratch_" + name, given[name].shape, F32, kind="Internal").ap()
    args["out"] = nc.dram_tensor("out_0", (T, S, D), F32, kind="ExternalOutput").ap()
    build(nc, args)
    r = run_bass_kernel_spmd(nc, [arrays], core_ids=[0])
    return r.results[0]["out_0"]
```
